# Optimizing a Trainium2 kernel written in Bass

```python
import numpy as np
import jax
import jax.numpy as jnp

def _softmax(x, axis=-1):
    return jax.nn.softmax(x, axis=axis)

def _gelu(x):
    return jax.nn.gelu(x, approximate=True)

def _silu(x):
    return jax.nn.silu(x)

def _sigmoid(x):
    return jax.nn.sigmoid(x)

def _layernorm(x, axis=-1, eps=1e-05):
    m = jnp.mean(x, axis=axis, keepdims=True)
    v = jnp.var(x, axis=axis, keepdims=True)
    return (x - m) / jnp.sqrt(v + eps)

def _scatter_add(tgt, idx, src, axis=0):
    return tgt.at[idx].add(src)

def _segment_sum(src, seg, n):
    return jax.ops.segment_sum(src, seg, n)
kernel_name = 'mk_conv_seq_d2_conv_nchw512_r2_78c13a'

def setup_inputs(seed: int=0):
    np.random.seed(seed)
    _w = jnp.asarray

    def _rec_inputs():
        import jax
        import jax.numpy as jnp
        _gk = jax.random.key(seed)
        x = -0.000929 + 1 * jax.random.normal(jax.random.fold_in(_gk, 1), (2, 256, 32, 32), jnp.float32)
        return x
    x = _rec_inputs()

    def _L0_conv_setup():
        import jax, jax.numpy as jnp
        import numpy as np
        B, C, H, W = (2, 256, 32, 32)
        HEADS = 8
        GROUPS = 8
        DH = 32
        DF = 4
        OFF_SCALE = 4.0
        EPS = 1e-05

        def _bn(t, gamma, beta):
            s = gamma / jnp.sqrt(1.0 + EPS)
            return t * s[None, :, None, None] + beta[None, :, None, None]

        def _gconv1x1(t, w):
            b, c, h, ww = t.shape
            o = jnp.einsum('bgci,goc->bgoi', t.reshape(b, GROUPS, c // GROUPS, h * ww), w)
            return o.reshape(b, GROUPS * w.shape[1], h, ww)

        def _grid_sample(img, grid):
            N, Ci, Hi, Wi = img.shape
            gx = (grid[..., 0] + 1.0) * (Wi / 2.0) - 0.5
            gy = (grid[..., 1] + 1.0) * (Hi / 2.0) - 0.5
            x0 = jnp.floor(gx)
            y0 = jnp.floor(gy)
            wx = gx - x0
            wy = gy - y0

            def gather(im, ix, iy):
                valid = (ix >= 0) & (ix < Wi) & (iy >= 0) & (iy < Hi)
                ixc = jnp.clip(ix, 0, Wi - 1).astype(jnp.int32)
                iyc = jnp.clip(iy, 0, Hi - 1).astype(jnp.int32)
                return im[:, iyc, ixc] * valid[None].astype(im.dtype)

            def sample_one(im, x0, y0, wx, wy):
                v00 = gather(im, x0, y0)
                v01 = gather(im, x0 + 1, y0)
                v10 = gather(im, x0, y0 + 1)
                v11 = gather(im, x0 + 1, y0 + 1)
                wx = wx[None]
                wy = wy[None]
                return v00 * (1 - wx) * (1 - wy) + v01 * wx * (1 - wy) + v10 * (1 - wx) * wy + v11 * wx * wy
            return jax.vmap(sample_one)(img, x0, y0, wx, wy)

        def _forward(x, bn1_g, bn1_b, bn2_g, bn2_b, qw, kw, vw, out_w, out_b, off_dw_w, off_dw_b, off_pw_w, cpb_w1, cpb_b1, cpb_w2, cpb_b2, cpb_w3, cpb_b3, mlp_w1, mlp_b1, mlp_w2, mlp_b2):
            b = x.shape[0]
            xn = _bn(x, bn1_g, bn1_b)
            q = _gconv1x1(xn, qw)
            qg = q.reshape(b * GROUPS, DH, H, W)
            off = jax.lax.conv_general_dilated(qg, off_dw_w, (DF, DF), ((1, 1), (1, 1)), dimension_numbers=('NCHW', 'OIHW', 'NCHW'), feature_group_count=DH)
            off = jax.nn.gelu(off + off_dw_b[None, :, None, None], approximate=False)
            off = jnp.tanh(jnp.einsum('bchw,oc->bohw', off, off_pw_w)) * OFF_SCALE
            Hd, Wd = (off.shape[-2], off.shape[-1])
            gy, gx = jnp.meshgrid(jnp.arange(Hd, dtype=x.dtype), jnp.arange(Wd, dtype=x.dtype), indexing='ij')
            vx = gx[None] + off[:, 0]
            vy = gy[None] + off[:, 1]
            nx = 2.0 * vx / max(Hd - 1, 1) - 1.0
            ny = 2.0 * vy / max(Wd - 1, 1) - 1.0
            vgrid_scaled = jnp.stack((nx, ny), axis=-1)
            kv = _grid_sample(xn.reshape(b * GROUPS, DH, H, W), vgrid_scaled)
            kv = kv.reshape(b, GROUPS * DH, Hd, Wd)
            k = _gconv1x1(kv, kw)
            v = _gconv1x1(kv, vw)
            scale = DH ** (-0.5)
            qh = q.reshape(b, HEADS, DH, H * W).transpose(0, 1, 3, 2) * scale
            kh = k.reshape(b, HEADS, DH, Hd * Wd).transpose(0, 1, 3, 2)
            vh = v.reshape(b, HEADS, DH, Hd * Wd).transpose(0, 1, 3, 2)
            qgy, qgx = jnp.meshgrid(jnp.arange(H, dtype=x.dtype), jnp.arange(W, dtype=x.dtype), indexing='ij')
            grid_q = jnp.stack((2.0 * qgx / max(H - 1, 1) - 1.0, 2.0 * qgy / max(W - 1, 1) - 1.0), axis=-1).reshape(1, H * W, 2)
            grid_kv = vgrid_scaled.reshape(b * GROUPS, Hd * Wd, 2)
            pos = grid_q[:, :, None, :] - grid_kv[:, None, :, :]
            bias = jnp.sign(pos) * jnp.log1p(jnp.abs(pos))
            bias = jax.nn.relu(bias @ cpb_w1 + cpb_b1)
            bias = jax.nn.relu(bias @ cpb_w2 + cpb_b2)
            bias = (bias @ cpb_w3 + cpb_b3).reshape(b, GROUPS, H * W, Hd * Wd)
            sim = jnp.einsum('bhid,bhjd->bhij', qh, kh) + bias
            attn = jax.nn.softmax(sim, axis=-1)
            out = jnp.einsum('bhij,bhjd->bhid', attn, vh)
            out = out.transpose(0, 1, 3, 2).reshape(b, HEADS * DH, H, W)
            out = jnp.einsum('bchw,oc->bohw', out, out_w) + out_b[None, :, None, None]
            x = x + out
            xn2 = _bn(x, bn2_g, bn2_b)
            h1 = jax.nn.gelu(jnp.einsum('bchw,oc->bohw', xn2, mlp_w1) + mlp_b1[None, :, None, None], approximate=False)
            return x + jnp.einsum('bchw,oc->bohw', h1, mlp_w2) + mlp_b2[None, :, None, None]
        ks = jax.random.split(jax.random.key(seed), 16)
        w = lambda k, shape: jax.random.normal(k, shape, dtype=jnp.float32) * 0.02
        return {'x': jax.random.normal(ks[0], (B, C, H, W), dtype=jnp.float32), 'bn1_g': jnp.ones((C,), jnp.float32), 'bn1_b': jnp.zeros((C,), jnp.float32), 'bn2_g': jnp.ones((C,), jnp.float32), 'bn2_b': jnp.zeros((C,), jnp.float32), 'qw': w(ks[1], (GROUPS, DH, C // GROUPS)), 'kw': w(ks[2], (GROUPS, DH, C // GROUPS)), 'vw': w(ks[3], (GROUPS, DH, C // GROUPS)), 'out_w': w(ks[4], (C, HEADS * DH)), 'out_b': jnp.zeros((C,), jnp.float32), 'off_dw_w': w(ks[5], (DH, 1, 6, 6)), 'off_dw_b': jnp.zeros((DH,), jnp.float32), 'off_pw_w': w(ks[6], (2, DH)), 'cpb_w1': w(ks[7], (2, 64)), 'cpb_b1': jnp.zeros((64,), jnp.float32), 'cpb_w2': w(ks[8], (64, 64)), 'cpb_b2': jnp.zeros((64,), jnp.float32), 'cpb_w3': w(ks[9], (64, 1)), 'cpb_b3': jnp.zeros((1,), jnp.float32), 'mlp_w1': w(ks[10], (4 * C, C)), 'mlp_b1': jnp.zeros((4 * C,), jnp.float32), 'mlp_w2': w(ks[11], (C, 4 * C)), 'mlp_b2': jnp.zeros((C,), jnp.float32)}
    _L0_conv_all = _L0_conv_setup()
    _L0_conv_in = {k: v for k, v in _L0_conv_all.items() if k in ('bn1_g', 'bn1_b', 'bn2_g', 'bn2_b', 'qw', 'kw', 'vw', 'out_w', 'out_b', 'off_dw_w', 'off_dw_b', 'off_pw_w', 'cpb_w1', 'cpb_b1', 'cpb_w2', 'cpb_b2', 'cpb_w3', 'cpb_b3', 'mlp_w1', 'mlp_b1', 'mlp_w2', 'mlp_b2')}
    del _L0_conv_all

    def _L1_conv_setup():
        import jax, jax.numpy as jnp
        import numpy as np
        N_HEADS = 8
        D_K = 32
        SCALE = D_K ** (-0.5)
        key = jax.random.key(seed)
        k1, k2, k3 = jax.random.split(key, 3)
        B, C, H, W = (8, 256, 32, 32)
        x = jax.random.normal(k1, (B, C, H, W), dtype=jnp.float32)
        W_qkv = jax.random.normal(k2, (C, N_HEADS * D_K * 3), dtype=jnp.float32) * (1.0 / np.sqrt(C))
        b_qkv = jnp.zeros((N_HEADS * D_K * 3,), dtype=jnp.float32)
        W_out = jax.random.normal(k3, (N_HEADS * D_K, C), dtype=jnp.float32) * (1.0 / np.sqrt(N_HEADS * D_K))
        b_out = jnp.zeros((C,), dtype=jnp.float32)
        return {'x': x, 'W_qkv': W_qkv, 'b_qkv': b_qkv, 'W_out': W_out, 'b_out': b_out}
    _L1_conv_all = _L1_conv_setup()
    _L1_conv_in = {k: v for k, v in _L1_conv_all.items() if k in ('W_qkv', 'b_qkv', 'W_out', 'b_out')}
    del _L1_conv_all
    return {'x': x, 'L0_conv_bn1_g': _L0_conv_in['bn1_g'], 'L0_conv_bn1_b': _L0_conv_in['bn1_b'], 'L0_conv_bn2_g': _L0_conv_in['bn2_g'], 'L0_conv_bn2_b': _L0_conv_in['bn2_b'], 'L0_conv_qw': _L0_conv_in['qw'], 'L0_conv_kw': _L0_conv_in['kw'], 'L0_conv_vw': _L0_conv_in['vw'], 'L0_conv_out_w': _L0_conv_in['out_w'], 'L0_conv_out_b': _L0_conv_in['out_b'], 'L0_conv_off_dw_w': _L0_conv_in['off_dw_w'], 'L0_conv_off_dw_b': _L0_conv_in['off_dw_b'], 'L0_conv_off_pw_w': _L0_conv_in['off_pw_w'], 'L0_conv_cpb_w1': _L0_conv_in['cpb_w1'], 'L0_conv_cpb_b1': _L0_conv_in['cpb_b1'], 'L0_conv_cpb_w2': _L0_conv_in['cpb_w2'], 'L0_conv_cpb_b2': _L0_conv_in['cpb_b2'], 'L0_conv_cpb_w3': _L0_conv_in['cpb_w3'], 'L0_conv_cpb_b3': _L0_conv_in['cpb_b3'], 'L0_conv_mlp_w1': _L0_conv_in['mlp_w1'], 'L0_conv_mlp_b1': _L0_conv_in['mlp_b1'], 'L0_conv_mlp_w2': _L0_conv_in['mlp_w2'], 'L0_conv_mlp_b2': _L0_conv_in['mlp_b2'], 'L1_conv_W_qkv': _L1_conv_in['W_qkv'], 'L1_conv_b_qkv': _L1_conv_in['b_qkv'], 'L1_conv_W_out': _L1_conv_in['W_out'], 'L1_conv_b_out': _L1_conv_in['b_out']}

def reference(x, L0_conv_bn1_g, L0_conv_bn1_b, L0_conv_bn2_g, L0_conv_bn2_b, L0_conv_qw, L0_conv_kw, L0_conv_vw, L0_conv_out_w, L0_conv_out_b, L0_conv_off_dw_w, L0_conv_off_dw_b, L0_conv_off_pw_w, L0_conv_cpb_w1, L0_conv_cpb_b1, L0_conv_cpb_w2, L0_conv_cpb_b2, L0_conv_cpb_w3, L0_conv_cpb_b3, L0_conv_mlp_w1, L0_conv_mlp_b1, L0_conv_mlp_w2, L0_conv_mlp_b2, L1_conv_W_qkv, L1_conv_b_qkv, L1_conv_W_out, L1_conv_b_out):
    import jax
    import jax.numpy as jnp

    def _L0_conv_ref(x, bn1_g, bn1_b, bn2_g, bn2_b, qw, kw, vw, out_w, out_b, off_dw_w, off_dw_b, off_pw_w, cpb_w1, cpb_b1, cpb_w2, cpb_b2, cpb_w3, cpb_b3, mlp_w1, mlp_b1, mlp_w2, mlp_b2):
        import jax, jax.numpy as jnp
        import numpy as np
        B, C, H, W = (2, 256, 32, 32)
        HEADS = 8
        GROUPS = 8
        DH = 32
        DF = 4
        OFF_SCALE = 4.0
        EPS = 1e-05

        def _bn(t, gamma, beta):
            s = gamma / jnp.sqrt(1.0 + EPS)
            return t * s[None, :, None, None] + beta[None, :, None, None]

        def _gconv1x1(t, w):
            b, c, h, ww = t.shape
            o = jnp.einsum('bgci,goc->bgoi', t.reshape(b, GROUPS, c // GROUPS, h * ww), w)
            return o.reshape(b, GROUPS * w.shape[1], h, ww)

        def _grid_sample(img, grid):
            N, Ci, Hi, Wi = img.shape
            gx = (grid[..., 0] + 1.0) * (Wi / 2.0) - 0.5
            gy = (grid[..., 1] + 1.0) * (Hi / 2.0) - 0.5
            x0 = jnp.floor(gx)
            y0 = jnp.floor(gy)
            wx = gx - x0
            wy = gy - y0

            def gather(im, ix, iy):
                valid = (ix >= 0) & (ix < Wi) & (iy >= 0) & (iy < Hi)
                ixc = jnp.clip(ix, 0, Wi - 1).astype(jnp.int32)
                iyc = jnp.clip(iy, 0, Hi - 1).astype(jnp.int32)
                return im[:, iyc, ixc] * valid[None].astype(im.dtype)

            def sample_one(im, x0, y0, wx, wy):
                v00 = gather(im, x0, y0)
                v01 = gather(im, x0 + 1, y0)
                v10 = gather(im, x0, y0 + 1)
                v11 = gather(im, x0 + 1, y0 + 1)
                wx = wx[None]
                wy = wy[None]
                return v00 * (1 - wx) * (1 - wy) + v01 * wx * (1 - wy) + v10 * (1 - wx) * wy + v11 * wx * wy
            return jax.vmap(sample_one)(img, x0, y0, wx, wy)

        def _forward(x, bn1_g, bn1_b, bn2_g, bn2_b, qw, kw, vw, out_w, out_b, off_dw_w, off_dw_b, off_pw_w, cpb_w1, cpb_b1, cpb_w2, cpb_b2, cpb_w3, cpb_b3, mlp_w1, mlp_b1, mlp_w2, mlp_b2):
            b = x.shape[0]
            xn = _bn(x, bn1_g, bn1_b)
            q = _gconv1x1(xn, qw)
            qg = q.reshape(b * GROUPS, DH, H, W)
            off = jax.lax.conv_general_dilated(qg, off_dw_w, (DF, DF), ((1, 1), (1, 1)), dimension_numbers=('NCHW', 'OIHW', 'NCHW'), feature_group_count=DH)
            off = jax.nn.gelu(off + off_dw_b[None, :, None, None], approximate=False)
            off = jnp.tanh(jnp.einsum('bchw,oc->bohw', off, off_pw_w)) * OFF_SCALE
            Hd, Wd = (off.shape[-2], off.shape[-1])
            gy, gx = jnp.meshgrid(jnp.arange(Hd, dtype=x.dtype), jnp.arange(Wd, dtype=x.dtype), indexing='ij')
            vx = gx[None] + off[:, 0]
            vy = gy[None] + off[:, 1]
            nx = 2.0 * vx / max(Hd - 1, 1) - 1.0
            ny = 2.0 * vy / max(Wd - 1, 1) - 1.0
            vgrid_scaled = jnp.stack((nx, ny), axis=-1)
            kv = _grid_sample(xn.reshape(b * GROUPS, DH, H, W), vgrid_scaled)
            kv = kv.reshape(b, GROUPS * DH, Hd, Wd)
            k = _gconv1x1(kv, kw)
            v = _gconv1x1(kv, vw)
            scale = DH ** (-0.5)
            qh = q.reshape(b, HEADS, DH, H * W).transpose(0, 1, 3, 2) * scale
            kh = k.reshape(b, HEADS, DH, Hd * Wd).transpose(0, 1, 3, 2)
            vh = v.reshape(b, HEADS, DH, Hd * Wd).transpose(0, 1, 3, 2)
            qgy, qgx = jnp.meshgrid(jnp.arange(H, dtype=x.dtype), jnp.arange(W, dtype=x.dtype), indexing='ij')
            grid_q = jnp.stack((2.0 * qgx / max(H - 1, 1) - 1.0, 2.0 * qgy / max(W - 1, 1) - 1.0), axis=-1).reshape(1, H * W, 2)
            grid_kv = vgrid_scaled.reshape(b * GROUPS, Hd * Wd, 2)
            pos = grid_q[:, :, None, :] - grid_kv[:, None, :, :]
            bias = jnp.sign(pos) * jnp.log1p(jnp.abs(pos))
            bias = jax.nn.relu(bias @ cpb_w1 + cpb_b1)
            bias = jax.nn.relu(bias @ cpb_w2 + cpb_b2)
            bias = (bias @ cpb_w3 + cpb_b3).reshape(b, GROUPS, H * W, Hd * Wd)
            sim = jnp.einsum('bhid,bhjd->bhij', qh, kh) + bias
            attn = jax.nn.softmax(sim, axis=-1)
            out = jnp.einsum('bhij,bhjd->bhid', attn, vh)
            out = out.transpose(0, 1, 3, 2).reshape(b, HEADS * DH, H, W)
            out = jnp.einsum('bchw,oc->bohw', out, out_w) + out_b[None, :, None, None]
            x = x + out
            xn2 = _bn(x, bn2_g, bn2_b)
            h1 = jax.nn.gelu(jnp.einsum('bchw,oc->bohw', xn2, mlp_w1) + mlp_b1[None, :, None, None], approximate=False)
            return x + jnp.einsum('bchw,oc->bohw', h1, mlp_w2) + mlp_b2[None, :, None, None]
        return _forward(x, bn1_g, bn1_b, bn2_g, bn2_b, qw, kw, vw, out_w, out_b, off_dw_w, off_dw_b, off_pw_w, cpb_w1, cpb_b1, cpb_w2, cpb_b2, cpb_w3, cpb_b3, mlp_w1, mlp_b1, mlp_w2, mlp_b2)

    def _L1_conv_ref(x, W_qkv, b_qkv, W_out, b_out):
        import jax, jax.numpy as jnp
        import numpy as np
        N_HEADS = 8
        D_K = 32
        SCALE = D_K ** (-0.5)
        B, C, H, W = x.shape
        N = H * W
        xf = jnp.transpose(x.reshape(B, C, N), (0, 2, 1))
        qkv = xf @ W_qkv + b_qkv
        qkv = qkv.reshape(B, N, N_HEADS, 3 * D_K)
        q, k, v = jnp.split(qkv, 3, axis=-1)
        attn = jnp.einsum('bihd,bjhd->bijh', q, k) * SCALE
        attn = jax.nn.softmax(attn, axis=2)
        res = jnp.einsum('bijh,bjhd->bihd', attn, v)
        res = res.reshape(B, N, N_HEADS * D_K)
        res = res @ W_out + b_out
        res = res + xf
        res = jnp.transpose(res, (0, 2, 1)).reshape(B, C, H, W)
        return res

    def _gn(v, G=32, eps=1e-05):
        B_, C_, H_, W_ = v.shape
        g = v.reshape(B_, G, C_ // G, H_, W_)
        m = jnp.mean(g, axis=(2, 3, 4), keepdims=True)
        s = jnp.var(g, axis=(2, 3, 4), keepdims=True)
        return ((g - m) / jnp.sqrt(s + eps)).reshape(v.shape)

    def _ln_c(v, eps=1e-06):
        m = jnp.mean(v, axis=1, keepdims=True)
        s = jnp.var(v, axis=1, keepdims=True)
        return (v - m) / jnp.sqrt(s + eps)

    def _ln_t(v, eps=1e-05):
        m = jnp.mean(v, axis=-1, keepdims=True)
        s = jnp.var(v, axis=-1, keepdims=True)
        return (v - m) / jnp.sqrt(s + eps)

    def _to_tokens(v):
        B_, C_, H_, W_ = v.shape
        return v.reshape(B_, C_, H_ * W_).transpose(0, 2, 1)

    def _from_tokens(t, like):
        B_, C_, H_, W_ = like.shape
        return t.transpose(0, 2, 1).reshape(B_, C_, H_, W_)
    x = _L0_conv_ref(x, L0_conv_bn1_g, L0_conv_bn1_b, L0_conv_bn2_g, L0_conv_bn2_b, L0_conv_qw, L0_conv_kw, L0_conv_vw, L0_conv_out_w, L0_conv_out_b, L0_conv_off_dw_w, L0_conv_off_dw_b, L0_conv_off_pw_w, L0_conv_cpb_w1, L0_conv_cpb_b1, L0_conv_cpb_w2, L0_conv_cpb_b2, L0_conv_cpb_w3, L0_conv_cpb_b3, L0_conv_mlp_w1, L0_conv_mlp_b1, L0_conv_mlp_w2, L0_conv_mlp_b2)
    x = _L1_conv_ref(x, L1_conv_W_qkv, L1_conv_b_qkv, L1_conv_W_out, L1_conv_b_out)
    return x

_drawn_inputs = setup_inputs


def setup_inputs(seed=0):
    import zlib

    import numpy as np

    out = dict(_drawn_inputs(seed))
    spreads = {'L0_conv_bn1_g': (1.0, 0.6),
     'L0_conv_bn1_b': (0.0, 0.8),
     'L0_conv_bn2_g': (1.0, 0.6),
     'L0_conv_bn2_b': (0.0, 0.499),
     'L0_conv_out_b': (0.0, 0.1),
     'L0_conv_off_dw_b': (0.0, 0.8),
     'L0_conv_cpb_b1': (0.0, 2.0),
     'L0_conv_cpb_b2': (0.0, 2.0),
     'L0_conv_mlp_b1': (0.0, 0.267),
     'L0_conv_mlp_b2': (0.0, 0.1),
     'L1_conv_b_qkv': (0.0, 0.1),
     'L1_conv_b_out': (0.0, 0.1)}
    factors = {'L0_conv_qw': 8.0,
     'L0_conv_kw': 8.0,
     'L0_conv_vw': 8.0,
     'L0_conv_out_w': 8.0,
     'L0_conv_off_dw_w': 8.0,
     'L0_conv_off_pw_w': 8.0,
     'L0_conv_cpb_w1': 8.0,
     'L0_conv_cpb_w2': 36.386,
     'L0_conv_cpb_w3': 38.473}
    for name, (base, spread) in spreads.items():
        noise = np.random.default_rng([zlib.crc32(name.encode()), seed]).standard_normal(out[name].shape)
        drawn = base * np.exp(spread * noise) if base else spread * noise
        out[name] = jnp.asarray(drawn.astype(out[name].dtype))
    for name, factor in factors.items():
        out[name] = (out[name] * factor).astype(out[name].dtype)
    return out
```

```python
import concourse.bass as bass
from concourse import mybir
from contextlib import ExitStack
import numpy as np

P = 128
B, C, H, W = 2, 256, 32, 32
N = H * W
CT = C // P
T = B * CT
NH, D = 8, 32
G = B * NH
HP = P // D
KD = 8
J = KD * KD
FT = 4 * C // P
TAPS, STRIDE = 6, 4
PADW, PADR = W + 2, 36
CH = 64
HALF = N // 2
NK = N // P
BN_INV = 1.0 / float(np.sqrt(np.float32(1.0 + 1e-5)))
SCALE = D ** -0.5

CHUNKS, STEPS = 8, 64
PARTS_S = [0, 0, 1, 1, 0, 2]
PARTS_W = [0, 1, 0, 1, 2, 0]
NR = len(PARTS_S)

Q_STACK = [[0, 0, 1, 1], [0, 2, 1, 2]]
K_STACK = [[0, 1, 0, 1], [2, 0, 2, 1]]

VEC = {}
_at = 0
for _n, _w in [("bn1_g", 2), ("bn1_b", 2), ("bn2_g", 2), ("bn2_b", 2), ("out_b", 2), ("mlp_b2", 2), ("b_out", 2),
               ("mlp_b1", 8), ("dw_w", 36), ("dw_b", 1), ("cb1", 1), ("cb2", 1), ("cb3", 1), ("pw", 2),
               ("bq", 2), ("bk", 2), ("px", 1), ("py", 8)]:
    VEC[_n] = (_at, _w)
    _at += _w
NVEC = _at


def build(nc, d, out):
    fp32, bf16 = mybir.dt.float32, mybir.dt.bfloat16
    ALU, ACT, AX = mybir.AluOpType, mybir.ActivationFunctionType, mybir.AxisListType

    ctx = ExitStack()
    with ctx:
        def sb(name, shape, dt=fp32):
            return ctx.enter_context(nc.sbuf_tensor(name, shape, dt))

        def sem(name):
            return ctx.enter_context(nc.semaphore(name))

        def dram(name, shape, dt):
            return nc.dram_tensor(name, shape, dt, kind="Internal").ap()

        grid_d = dram("grid_d", [2 * G, J], fp32)
        s_d = dram("s_d", [3, 2, G, J * W], bf16)
        w1_d = dram("w1_d", [2, 3, CH], bf16)
        q_d = dram("q_d", [3, G * D, N], bf16)
        k_d = dram("k_d", [3, G * D, N], bf16)

        vec = sb("vec", [P, NVEC])
        ident = sb("ident", [P, P])
        gridj = sb("gridj", [2 * G, J])
        gridq = sb("gridq", [2 * G, W])
        X = sb("X", [P, T, N])
        XN = sb("XN", [P, T, N])
        qpad = sb("qpad", [P, T * PADR + 4, PADW])
        qw = sb("qw", [P, CT, P])
        kw = sb("kw", [P, CT, P])
        vw = sb("vw", [P, CT, P])
        outw = sb("outw", [P, CT, C])
        m1 = sb("m1", [P, CT, 4 * C])
        m2 = sb("m2", [P, FT, C])
        wqkv = sb("wqkv", [P, CT, 3 * C])
        wout = sb("wout", [P, CT, C])
        bv = sb("bv", [P, NH, D])
        sc = sb("sc", [P, 4])
        conv = sb("conv", [P, T * 9, KD])
        gel = sb("gel", [P, T * 9, KD])
        pwl = sb("pwl", [P, T, 2, G])
        off = sb("off", [2 * G, J])
        vpos = sb("vpos", [2 * G, J])
        npos = sb("npos", [2 * G, J])
        gxy = sb("gxy", [2 * G, J])
        w1s = sb("w1s", [2, CH])
        w1r = sb("w1r", [2, CH])
        w1p = sb("w1p", [2, 3, CH], bf16)
        wl1 = sb("wl1", [P, P], bf16)
        w2bd = sb("w2bd", [P, P])
        w3bd = sb("w3bd", [P, 2])
        sx = sb("sx", [P, G + 1, CHUNKS, W], bf16)
        sy = sb("sy", [P, G + 1, CHUNKS, W], bf16)
        SIM = sb("SIM", [P, G, NK * J])
        big = sb("big", [P, 12, N])
        kvs = sb("kvs", [P, T, J])
        ks = sb("ks", [P, T, J])
        vs = sb("vs", [J, T, P])
        mv = [sb(f"mv{i}", [P, N], bf16) for i in range(2)]
        gb = sb("gb", [P, 2, G * J])
        hx = sb("hx", [P, G * J])
        h1 = [gb[:, i // 2, HALF * (i % 2):HALF * (i % 2 + 1)] for i in range(4)]
        h2 = [hx[:, HALF * i:HALF * (i + 1)] for i in range(2)]
        smax = sb("smax", [P, HP * NK])
        ssum = sb("ssum", [P, HP * NK])
        srec = sb("srec", [P, HP * NK])

        pos = SIM[0:2 * G, 0:4, :].rearrange("p a b -> p (a b)")
        pp = SIM[0:2 * G, 4:8, :].rearrange("p a b -> p (a b)")
        pn = SIM[0:2 * G, 8:12, :].rearrange("p a b -> p (a b)")
        s3 = SIM[0:2 * G, 12:16, :].rearrange("p a b -> p (a b)")
        xnT = big[:, 0:4, :]
        wsm = big[:, 4:12, :]
        att = [big[0:J, i, :] for i in (0, 1)]
        ao = big[:, 2:6, :]
        hm = big[:, 6:10, :].rearrange("p a b -> p (a b)").rearrange("p (f n) -> p f n", f=FT)
        spt = [gb[0:2 * G, 0, :].bitcast(bf16), gb[0:2 * G, 1, :].bitcast(bf16), hx[0:2 * G, :].bitcast(bf16)]

        ps = ctx.enter_context(nc.psum_tensor("ps", [P, 8 * 512], fp32))

        def bank(i, n=1):
            return ps[:, 512 * i:512 * (i + n)]

        def v(name, i=0, n=1):
            a = VEC[name][0] + i
            return vec[:, a:a + n]

        ld_vec, ld_bd, ld_w1, ld_late = (sem(x) for x in ("ld_vec", "ld_bd", "ld_w1", "ld_late"))
        ld_x = [sem(f"ld_x{b}") for b in range(B)]
        cleared = sem("cleared")
        dve_chain = sem("dve_chain")
        scales_ready, xn_ready, q_ready, q_saved = (sem(x) for x in ("scales_ready", "xn_ready", "q_ready", "q_saved"))
        xT_ready, xT_saved, conv_ready, gelu_ready = (sem(x) for x in ("xT_ready", "xT_saved", "conv_ready", "gelu_ready"))
        pwl_ready, pw_ready, off_ready, gxy_ready = (sem(x) for x in ("pwl_ready", "pw_ready", "off_ready", "gxy_ready"))
        grid_out, grid_in, w1p_ready, w1_out, w1_in = (sem(x) for x in ("grid_out", "grid_in", "w1p_ready", "w1_out", "w1_in"))
        pn_ready, ln_ready, sparts_ready, s_out, s_in = (sem(x) for x in ("pn_ready", "ln_ready", "sparts_ready", "s_out", "s_in"))
        ws_ready, kv_ready, kv_saved, k_ready, v_ready, k_saved, v_saved = (
            sem(x) for x in ("ws_ready", "kv_ready", "kv_saved", "k_ready", "v_ready", "k_saved", "v_saved"))
        abs_ready, hat_ready = sem("abs_ready"), sem("hat_ready")
        q_copied, qk_ready, qk_saved = sem("q_copied"), sem("qk_ready"), sem("qk_saved")
        mv_ready, z1_ready, h1_ready, z2_ready, h2_ready, bias_ready, bias_saved = (
            sem(x) for x in ("mv_ready", "z1_ready", "h1_ready", "z2_ready", "h2_ready", "bias_ready", "bias_saved"))
        shifted, exped, normed, aT_ready, aT_saved, o_ready, o_saved = (
            sem(x) for x in ("shifted", "exped", "normed", "aT_ready", "aT_saved", "o_ready", "o_saved"))
        y_ready, x1_ready, xn2_ready, hid_ready, hid_saved, m_ready, x2_ready = (
            sem(x) for x in ("y_ready", "x1_ready", "xn2_ready", "hid_ready", "hid_saved", "m_ready", "x2_ready"))
        p_ready, f_ready, f_hi, f_res, f_mid, f_lo = (
            sem(x) for x in ("p_ready", "f_ready", "f_hi", "f_res", "f_mid", "f_lo"))
        parts_out = [sem("parts_out0"), sem("parts_out1")]
        max_done, rec_done = sem("max_done"), sem("rec_done")
        vv_ready, vv_saved = sem("vv_ready"), sem("vv_saved")
        st_in = [sem("st_in0"), sem("st_in1")]
        sc_ready, mx_ready, pr_ready, pT_ready, pTa_saved, pTd_saved, oo_ready, oo_saved = (
            sem(x) for x in ("sc_ready", "mx_ready", "pr_ready", "pT_ready", "pTa_saved", "pTd_saved", "oo_ready", "oo_saved"))
        rT_ready, rT_saved, fin_ready, fin_saved, stored = (
            sem(x) for x in ("rT_ready", "rT_saved", "fin_ready", "fin_saved", "stored"))

        V = big[:, 0:4, :].rearrange("p a b -> p (a b)").rearrange("p (j n d) -> p j n d", j=NK, n=G)
        RES = big[:, 4:8, :].rearrange("p a b -> p (a b)").rearrange("p (i n d) -> p i n d", i=NK, n=G)
        rT = XN
        PR = [big[:, 8, :], big[:, 9, :]]
        PTS = [big[:, 10, :], big[:, 11, :]]
        F = [SIM[:, 0:2, :].rearrange("p a b -> p (a b)"), SIM[:, 2:4, :].rearrange("p a b -> p (a b)")]
        R = [SIM[:, 4:6, :].rearrange("p a b -> p (a b)"), SIM[:, 6:8, :].rearrange("p a b -> p (a b)")]
        part = [[SIM[:, 8 + 3 * i + a, :].bitcast(bf16) for a in range(3)] for i in range(2)]
        QS = [[SIM[:, 4 * i + a, :].bitcast(bf16) for a in range(2)] for i in range(2)]
        KS = [[SIM[:, 4 * i + 2 + a, :].bitcast(bf16) for a in range(2)] for i in range(2)]
        amax = [sb(f"amax{i}", [P, 1]) for i in range(2)]
        aneg = [sb(f"aneg{i}", [P, 1]) for i in range(2)]
        asum = [sb(f"asum{i}", [P, 1]) for i in range(4)]
        arec = [sb(f"arec{i}", [P, 1]) for i in range(2)]

        out_v = out.rearrange("b (c p) n -> p b c n", p=P)
        x_v = d["x"].rearrange("b (c p) n -> p b c n", p=P)

        block = ctx.enter_context(nc.Block())

        @block.sync
        def _(sp):
            sp.dma_start(vec[:, :], d["vecs"]).then_inc(ld_vec, 16)
            for b in range(B):
                sp.dma_start(X[:, CT * b:CT * (b + 1), :], x_v[:, b]).then_inc(ld_x[b], 16)
            sp.dma_start(ident[:, :], d["ident"]).then_inc(ld_vec, 16)
            sp.dma_start(gridj[:, :], d["gridj"]).then_inc(ld_vec, 16)
            sp.dma_start(gridq[:, :], d["gridq"]).then_inc(ld_vec, 16)
            sp.wait_ge(cleared, 6)
            for w, src in ((qw, "qwT"), (kw, "kwT"), (vw, "vwT")):
                for h in range(HP):
                    sp.dma_start(w[D * h:D * (h + 1), :, D * h:D * (h + 1)],
                                 d[src].rearrange("(t h) c o -> h c t o", h=HP)[h]).then_inc(ld_bd, 16)
            for h in range(2):
                sp.dma_start(w2bd[CH * h:CH * (h + 1), CH * h:CH * (h + 1)], d["cw2"]).then_inc(ld_bd, 16)
                sp.dma_start(w3bd[CH * h:CH * (h + 1), h:h + 1], d["cw3"]).then_inc(ld_bd, 16)
            sp.wait_ge(w1p_ready, 1)
            sp.dma_start(w1_d, w1p[:, :, :]).then_inc(w1_out, 16)
            sp.wait_ge(w1_out, 16)
            for jh in range(2):
                for c in range(2):
                    for r in range(NR):
                        row = 2 * NR * jh + NR * c + r
                        sp.dma_start(wl1[row:row + 97:32, CH * jh:CH * (jh + 1)],
                                     w1_d[c, PARTS_W[r]:PARTS_W[r] + 1, :].to_broadcast((4, CH))).then_inc(w1_in, 16)
            sp.wait_ge(gxy_ready, 1)
            sp.dma_start(grid_d, gxy[:, :]).then_inc(grid_out, 16)
            sp.wait_ge(sparts_ready, 3)
            for a in range(3):
                sp.dma_start(s_d[a].rearrange("c g n -> (c g) n"), spt[a]).then_inc(s_out, 16)
            sp.wait_ge(s_out, 48)
            sp.wait_ge(cleared, 10)
            sv = s_d.rearrange("a c g (h q n) -> a c h q g n", h=2, q=4)
            for jh in range(2):
                for c in range(2):
                    for r in range(NR):
                        row = 2 * NR * jh + NR * c + r
                        dst = (sx, sy)[c]
                        sp.dma_start(dst[row:row + 97:32, 0:G, :, :].rearrange("p g a b -> p g (a b)"),
                                     sv[PARTS_S[r], c, jh]).then_inc(s_in, 16)
            sp.wait_ge(grid_out, 16)
            sp.dma_start(gb[:, :, :].rearrange("p a b -> p (a b)"),
                         grid_d.rearrange("a b -> (a b)").partition_broadcast(P)).then_inc(grid_in, 16)
            for dst, src, n in ((outw, "out_wT", CT), (m1, "m1T", CT), (m2, "m2T", FT), (wqkv, "wqkv", CT), (wout, "wout", CT)):
                sp.dma_start(dst[:, :, :], d[src].rearrange("(t p) n -> p t n", p=P)).then_inc(ld_late, 16)
            sp.dma_start(bv[:, :, :], d["bv"].partition_broadcast(P)).then_inc(ld_late, 16)

            for n in range(2 * T):
                which, t = n // T, n % T
                dst = (q_d, k_d)[which]
                for a, s in enumerate((f_hi, f_mid, f_lo)):
                    sp.wait_ge(s, n + 1)
                    sp.dma_start(dst[a, P * t:P * (t + 1), :], part[n % 2][a]).then_inc(parts_out[n % 2], 16)

            def load_head(i, n):
                for st in range(2):
                    for r in range(HP):
                        sp.dma_start(QS[i][st][D * r:D * (r + 1), :],
                                     q_d[Q_STACK[st][r], bass.ds(n * D, D), :]).then_inc(st_in[i], 16)
                        sp.dma_start(KS[i][st][D * r:D * (r + 1), :],
                                     k_d[K_STACK[st][r], bass.ds(n * D, D), :]).then_inc(st_in[i], 16)

            for i in range(2):
                sp.wait_ge(parts_out[i], 48 * T)
            load_head(0, 0)
            load_head(1, 1)
            with sp.Fori(0, G // 2 - 1) as k:
                sp.wait_ge(sc_ready, 16 * k + 8)
                load_head(0, 2 * k + 2)
                sp.wait_ge(sc_ready, 16 * k + 16)
                load_head(1, 2 * k + 3)

            for n in range(T):
                for hf in range(2):
                    sp.wait_ge(fin_saved, 2 * n + hf + 1)
                    sp.dma_start(out_v[:, n // CT, n % CT, HALF * hf:HALF * (hf + 1)],
                                 X[:, n, HALF * hf:HALF * (hf + 1)]).then_inc(stored, 16)
            sp.wait_ge(stored, 16 * 2 * T)

        @block.gpsimd
        def _(pool):
            for m in (qw[:, :, :], kw[:, :, :], vw[:, :, :], w3bd[:, :], w2bd[:, :], wl1[:, :],
                      qpad[:, :, :], pwl[:, :, :, :], sx[:, :, :, :], sy[:, :, :, :]):
                pool.memset(m, 0.0).then_inc(cleared, 1)

            def spread(i, g, jj):
                shape = (P, H, W)
                pool.tensor_tensor(mv[i][:, :].rearrange("p (a b) -> p a b", a=H),
                                   sx[:, g, jj, :].unsqueeze(1).to_broadcast(shape),
                                   sy[:, g, jj, :].unsqueeze(2).to_broadcast(shape), ALU.add).then_inc(mv_ready, 1)

            pool.wait_ge(q_saved, 2 * T)
            pool.wait_ge(xT_ready, 2 * T)
            for t in range(T):
                row = PADR * t + 1
                pool.tensor_copy(XN[:, t, :].rearrange("p (a b) -> p a b", b=W), qpad[:, row:row + H, 1:1 + W]).then_inc(q_copied, 1)

            pool.wait_ge(s_in, 16 * 4 * NR)
            spread(0, 0, 0)
            with pool.Fori(0, G) as g:
                for c in range(1, CHUNKS + 1):
                    pool.wait_ge(z1_ready, STEPS * g + max(8 * (c - 1), 1))
                    spread(c % 2, g + c // CHUNKS, c % CHUNKS)

        @block.scalar
        def _(act):
            act.dma_start(w1s[:, :], d["cw1"]).then_inc(ld_w1, 16)
            act.wait_ge(scales_ready, 1)
            for t in range(T):
                act.wait_ge(ld_x[t // CT], 16)
                act.activation(XN[:, t, :], X[:, t, :], ACT.Identity, scale=sc[:, t % CT:t % CT + 1],
                               bias=v("bn1_b", t % CT)).then_inc(xn_ready, 1)
            for r in range(2 * T):
                act.wait_ge(xT_ready, r + 1)
                act.activation(xnT[:, r // 2, HALF * (r % 2):HALF * (r % 2 + 1)], bank(r), ACT.Identity).then_inc(xT_saved, 1)
            act.wait_ge(conv_ready, 1)
            act.activation(gel[:, :, :], conv[:, :, :], ACT.Gelu, bias=v("dw_b")).then_inc(gelu_ready, 1)
            act.wait_ge(pw_ready, 1)
            act.activation(off[:, :], ps[0:2 * G, 0:J], ACT.Tanh).then_inc(off_ready, 1)
            act.wait_ge(pn_ready, 1)
            act.activation(pp, pp, ACT.Ln, bias=1.0).then_inc(ln_ready, 1)
            act.wait_ge(pn_ready, 2)
            act.activation(pn, pn, ACT.Ln, bias=1.0).then_inc(ln_ready, 1)
            act.wait_ge(grid_in, 16)
            for i in range(NK + 1):
                dst, src, pixel = (hx[:, :], gb[:, 0, :], v("px")) if i == 0 else (wsm[:, i - 1, :], gb[:, 1, :], v("py", i - 1))
                act.activation(dst, src, ACT.Abs, scale=-1.0, bias=pixel).then_inc(abs_ready, 1)
                act.wait_ge(abs_ready, i + 1)
                act.activation(dst, dst, ACT.Relu, scale=-1.0, bias=1.0).then_inc(hat_ready, 1)
            act.wait_ge(kv_ready, 1)
            act.activation(kvs[:, :, :], bank(1)[:, 0:T * J].rearrange("p (t j) -> p t j", t=T), ACT.Identity).then_inc(kv_saved, 1)
            act.wait_ge(k_ready, 1)
            act.activation(ks[:, :, :], bank(2)[:, 0:T * J].rearrange("p (t j) -> p t j", t=T), ACT.Identity,
                           scale=SCALE).then_inc(k_saved, 1)
            act.wait_ge(v_ready, 1)
            act.activation(vs[:, :, :], ps[0:J, 512 * 3:512 * 4].rearrange("p (t o) -> p t o", t=T), ACT.Identity).then_inc(v_saved, 1)
            act.wait_ge(s_out, 48)
            for g in range(G):
                act.wait_ge(qk_ready, g + 1)
                act.activation(SIM[:, g, :], bank(4 + g % 4), ACT.Identity).then_inc(qk_saved, 1)

            for s in range(2):
                act.wait_ge(z1_ready, s + 1)
                act.activation(h1[s], bank(s), ACT.Relu, bias=v("cb1")).then_inc(h1_ready, 1)
            with act.Fori(0, G) as g:
                for s in range(2, STEPS + 2):
                    act.wait_ge(z1_ready, STEPS * g + s + 1)
                    act.activation(h1[s % 4], bank(s % 2), ACT.Relu, bias=v("cb1")).then_inc(h1_ready, 1)

            for t in range(T):
                act.wait_ge(shifted, t + 1)
                act.activation(SIM[:, HP * t:HP * (t + 1), :], SIM[:, HP * t:HP * (t + 1), :], ACT.Exp).then_inc(exped, 1)
            for g in range(G):
                act.wait_ge(aT_ready, g + 1)
                act.activation(att[g % 2], ps[0:J, 1024 * (g % 2):1024 * (g % 2) + N], ACT.Identity).then_inc(aT_saved, 1)
                if g % HP == HP - 1:
                    t = g // HP
                    act.wait_ge(o_ready, t + 1)
                    act.activation(ao[:, t, :], bank(4 + 2 * (t % 2), 2), ACT.Identity).then_inc(o_saved, 1)
            for n in range(T):
                for ct in range(CT):
                    b, hf = n // 2, n % 2
                    act.wait_ge(x1_ready, CT * n + ct + 1)
                    act.activation(XN[:, CT * b + ct, HALF * hf:HALF * (hf + 1)], X[:, CT * b + ct, HALF * hf:HALF * (hf + 1)],
                                   ACT.Identity, scale=sc[:, CT + ct:CT + ct + 1], bias=v("bn2_b", ct)).then_inc(xn2_ready, 1)
            for n in range(T):
                for f in range(FT):
                    act.wait_ge(hid_ready, FT * n + f + 1)
                    act.activation(hm[:, f, :], bank(f % 4), ACT.Gelu, bias=v("mlp_b1", f)).then_inc(hid_saved, 1)

            for n in range(2 * T):
                which, t = n // T, n % T
                i = n % 2
                act.wait_ge(p_ready, n + 1)
                if n >= 2:
                    act.wait_ge(f_lo, n - 1)
                    act.wait_ge(parts_out[i], 48 * (n // 2))
                act.activation(F[i], bank(2 * i, 2), ACT.Identity, bias=v(("bq", "bk")[which], t % CT)).then_inc(f_ready, 1)
                act.wait_ge(f_ready, n + 1)
                act.activation(part[i][0], F[i], ACT.Copy).then_inc(f_hi, 1)
                act.wait_ge(f_res, n + 1)
                act.activation(part[i][1], R[i], ACT.Copy).then_inc(f_mid, 1)

            with act.Fori(0, G // 2) as k:
                for u in range(16):
                    act.wait_ge(mx_ready, 16 * k + u + 1)
                    act.activation(PR[u % 2], bank(2 * (u % 2), 2), ACT.Exp, scale=SCALE, bias=aneg[u % 2][:, :],
                                   accum_out=asum[u % 4][:, :]).then_inc(pr_ready, 1)
                    act.wait_ge(pT_ready, 16 * k + u + 1)
                    act.activation(PTS[u % 2][:, 0:HALF], bank(4), ACT.Identity).then_inc(pTa_saved, 1)
            for n in range(2 * T):
                act.wait_ge(rT_ready, n + 1)
                act.activation(rT[:, n // 2, HALF * (n % 2):HALF * (n % 2 + 1)], bank(n % 4), ACT.Identity).then_inc(rT_saved, 1)

        @block.vector
        def _(dve):
            chain = [0]

            def link(ins):
                chain[0] += 1
                ins.then_inc(dve_chain, 1)
                dve.wait_ge(dve_chain, chain[0])

            dve.wait_ge(ld_vec, 64)
            dve.tensor_scalar(sc[:, 0:CT], v("bn1_g", 0, CT), BN_INV, None, ALU.mult).then_inc(scales_ready, 1)
            dve.tensor_scalar(sc[:, CT:2 * CT], v("bn2_g", 0, CT), BN_INV, None, ALU.mult)
            dve.wait_ge(ld_w1, 16)
            link(dve.tensor_copy(w1p[:, 0, :], w1s[:, :]))
            link(dve.tensor_tensor(w1r[:, :], w1s[:, :], w1p[:, 0, :], ALU.subtract))
            link(dve.tensor_copy(w1p[:, 1, :], w1r[:, :]))
            dve.tensor_tensor(w1p[:, 2, :], w1r[:, :], w1p[:, 1, :], ALU.subtract).then_inc(w1p_ready, 1)
            dve.wait_ge(cleared, 8)
            for h in range(HP):
                for t in range(T):
                    last = dve.tensor_copy(pwl[D * h:D * (h + 1), t, :, HP * t + h], vec[D * h:D * (h + 1), VEC["pw"][0]:VEC["pw"][0] + 2])
            last.then_inc(pwl_ready, 1)
            for r in range(2 * T):
                t, hf = r // 2, r % 2
                dve.wait_ge(q_ready, r + 1)
                row = PADR * t + 1 + (H // 2) * hf
                dve.tensor_copy(qpad[:, row:row + H // 2, 1:1 + W], bank(r).rearrange("p (a b) -> p a b", b=W)).then_inc(q_saved, 1)
            dve.wait_ge(q_saved, 2 * T)
            for tap in range(TAPS * TAPS):
                ky, kx = tap // TAPS, tap % TAPS
                src = qpad[:, ky:ky + STRIDE * (T * 9 - 1) + 1:STRIDE, kx:kx + STRIDE * (KD - 1) + 1:STRIDE]
                if tap == 0:
                    link(dve.tensor_scalar(conv[:, :, :], src, v("dw_w", 0), None, ALU.mult))
                else:
                    link(dve.scalar_tensor_tensor(conv[:, :, :], src, v("dw_w", tap), conv[:, :, :], ALU.mult, ALU.add))
            dve.sem_inc(conv_ready, 1)
            dve.wait_ge(off_ready, 1)
            link(dve.scalar_tensor_tensor(vpos[:, :], off[:, :], 4.0, gridj[:, :], ALU.mult, ALU.add))
            link(dve.tensor_scalar(npos[:, :], vpos[:, :], 2.0 / (KD - 1), -1.0, ALU.mult, ALU.add))
            link(dve.tensor_scalar(gxy[:, :], npos[:, :], 1.0, W / 2.0, ALU.add, ALU.mult))
            link(dve.tensor_scalar(gxy[:, :], gxy[:, :], -0.5, None, ALU.add))
            dve.sem_inc(gxy_ready, 1)
            shape = (2 * G, J, W)
            r3 = "p (j q) -> p j q"
            link(dve.tensor_tensor(pos.rearrange(r3, j=J), gridq[:, :].unsqueeze(1).to_broadcast(shape),
                                   npos[:, :].unsqueeze(2).to_broadcast(shape), ALU.subtract))
            dve.tensor_scalar(pp, pos, 0.0, None, ALU.max).then_inc(pn_ready, 1)
            dve.tensor_scalar(pn, pos, -1.0, 0.0, ALU.mult, ALU.max).then_inc(pn_ready, 1)
            dve.wait_ge(ln_ready, 2)
            link(dve.tensor_tensor(s3, pp, pn, ALU.subtract))
            link(dve.tensor_copy(spt[0], s3))
            link(dve.tensor_tensor(pos, s3, spt[0], ALU.subtract))
            link(dve.tensor_copy(spt[1], pos))
            dve.tensor_tensor(spt[2], pos, spt[1], ALU.subtract).then_inc(sparts_ready, 3)
            dve.wait_ge(hat_ready, 1)
            for k in range(NK):
                dve.wait_ge(hat_ready, k + 2)
                dve.tensor_tensor(wsm[:, k, :], wsm[:, k, :], hx[:, :], ALU.mult).then_inc(ws_ready, 1)

            dve.wait_ge(qk_saved, G)
            dve.sem_inc(bias_saved, 1)
            with dve.Fori(0, G) as g:
                for s in range(STEPS):
                    dve.wait_ge(z2_ready, STEPS * g + s + 1)
                    dve.tensor_scalar(h2[s % 2], bank(2 + s % 2), v("cb2"), 0.0, ALU.add, ALU.max).then_inc(h2_ready, 1)
                dve.wait_ge(bias_ready, g + 1)
                dve.tensor_tensor(SIM[:, g, :], bank(4), SIM[:, g, :], ALU.add).then_inc(bias_saved, 1)
            dve.wait_ge(bias_saved, G + 1)

            for t in range(T):
                s = SIM[:, HP * t:HP * (t + 1), :].rearrange("p g (i j) -> p (g i) j", j=J)
                shape = (P, HP * NK, J)
                link(dve.tensor_reduce(smax[:, :], s, AX.X, ALU.max))
                link(dve.tensor_scalar(smax[:, :], smax[:, :], v("cb3"), None, ALU.add))
                dve.scalar_tensor_tensor(s, s, v("cb3"), smax[:, :].unsqueeze(2).to_broadcast(shape),
                                         ALU.add, ALU.subtract).then_inc(shifted, 1)
                dve.wait_ge(exped, t + 1)
                link(dve.tensor_reduce(ssum[:, :], s, AX.X, ALU.add))
                link(dve.reciprocal(srec[:, :], ssum[:, :]))
                dve.tensor_tensor(s, s, srec[:, :].unsqueeze(2).to_broadcast(shape), ALU.mult).then_inc(normed, 1)
            for n in range(T):
                b, hf = n // 2, n % 2
                for ct in range(CT):
                    r = CT * n + ct
                    xs = X[:, CT * b + ct, HALF * hf:HALF * (hf + 1)]
                    dve.wait_ge(y_ready, r + 1)
                    dve.scalar_tensor_tensor(xs, bank(r % 4), v("out_b", ct), xs, ALU.add, ALU.add).then_inc(x1_ready, 1)
            for n in range(T):
                b, hf = n // 2, n % 2
                for ct in range(CT):
                    r = CT * n + ct
                    xs = X[:, CT * b + ct, HALF * hf:HALF * (hf + 1)]
                    dve.wait_ge(m_ready, r + 1)
                    dve.wait_ge(xn2_ready, r + 1)
                    dve.scalar_tensor_tensor(xs, bank(4 + r % 4), v("mlp_b2", ct), xs, ALU.add, ALU.add).then_inc(x2_ready, 1)
            for n in range(2 * NK):
                b, jt = n // NK, n % NK
                dve.wait_ge(vv_ready, n + 1)
                dve.tensor_tensor(V[:, jt, NH * b:NH * (b + 1), :], bank(4 + n % 4)[:, 0:C].rearrange("p (n d) -> p n d", d=D),
                                  bv[:, :, :], ALU.add).then_inc(vv_saved, 1)
            for n in range(2 * T):
                i = n % 2
                dve.wait_ge(f_hi, n + 1)
                dve.tensor_tensor(R[i], F[i], part[i][0], ALU.subtract).then_inc(f_res, 1)
                dve.wait_ge(f_mid, n + 1)
                dve.tensor_tensor(part[i][2], R[i], part[i][1], ALU.subtract).then_inc(f_lo, 1)

            dve.sem_inc(oo_saved, 1)
            with dve.Fori(0, G // 2) as k:
                def move(u):
                    dve.wait_ge(pT_ready, 16 * k + u + 1)
                    dve.tensor_copy(PTS[u % 2][:, HALF:N], bank(5)).then_inc(pTd_saved, 1)

                def norm(u):
                    dve.wait_ge(oo_ready, 16 * k + u + 1)
                    dve.reciprocal(arec[u % 2][:, :], asum[u % 4][:, :]).then_inc(rec_done, 1)
                    dve.wait_ge(rec_done, 16 * k + u + 1)
                    dve.tensor_scalar(RES[:, u % NK, 2 * k + u // NK, :], bank(6 + u % 2)[:, 0:D], arec[u % 2][:, :], None,
                                      ALU.mult).then_inc(oo_saved, 1)

                for u in range(16):
                    dve.wait_ge(sc_ready, 16 * k + u + 1)
                    dve.tensor_reduce(amax[u % 2][:, :], bank(2 * (u % 2), 2), AX.X, ALU.max).then_inc(max_done, 1)
                    dve.wait_ge(max_done, 16 * k + u + 1)
                    dve.tensor_scalar(aneg[u % 2][:, :], amax[u % 2][:, :], -SCALE, None, ALU.mult).then_inc(mx_ready, 1)
                    if u >= 1:
                        move(u - 1)
                    if u >= 2:
                        norm(u - 2)
                move(15)
                for u in (14, 15):
                    norm(u)
            for n in range(2 * T):
                b, ct, hf = n // 4, n // 2 % 2, n % 2
                xs = X[:, CT * b + ct, HALF * hf:HALF * (hf + 1)]
                dve.wait_ge(fin_ready, n + 1)
                dve.scalar_tensor_tensor(xs, bank(4 + n % 4), v("b_out", ct), xs, ALU.add, ALU.add).then_inc(fin_saved, 1)

        @block.tensor
        def _(pe):
            pe.wait_ge(ld_bd, 16 * (3 * HP + 4))
            for t in range(T):
                pe.wait_ge(xn_ready, t + 1)
                for hf in range(2):
                    pe.matmul(bank(2 * t + hf), qw[:, t % CT, :], XN[:, t, HALF * hf:HALF * (hf + 1)],
                              start=True, stop=True).then_inc(q_ready, 1)
            pe.wait_ge(ld_vec, 64)
            for r in range(2 * T):
                pe.wait_ge(q_saved, r + 1)
                for i in range(4):
                    k = 4 * (r % 2) + i
                    last = pe.transpose(bank(r)[:, P * i:P * (i + 1)], XN[:, r // 2, P * k:P * (k + 1)], ident[:, :])
                last.then_inc(xT_ready, 1)
            pe.wait_ge(gelu_ready, 1)
            pe.wait_ge(pwl_ready, 1)
            pe.wait_ge(xT_saved, 2 * T)
            for t in range(T):
                last = pe.matmul(ps[0:2 * G, 0:J], pwl[:, t, :, :].rearrange("p c g -> p (c g)"), gel[:, 9 * t:9 * t + KD, :],
                                 start=(t == 0), stop=(t == T - 1))
            last.then_inc(pw_ready, 1)
            for k in range(NK):
                pe.wait_ge(ws_ready, k + 1)
                for t in range(T):
                    for h in range(HP):
                        g = HP * t + h
                        last = pe.matmul(ps[D * h:D * (h + 1), 512 + J * t:512 + J * (t + 1)],
                                         xnT[:, t, P * k + D * h:P * k + D * (h + 1)], wsm[:, k, J * g:J * (g + 1)],
                                         start=(k == 0 and t == 0), stop=(k == NK - 1), skip_group_check=True)
            last.then_inc(kv_ready, 1)
            pe.wait_ge(kv_saved, 1)
            for t in range(T):
                last = pe.matmul(bank(2)[:, J * t:J * (t + 1)], kw[:, t % CT, :], kvs[:, t, :], start=True, stop=True)
            last.then_inc(k_ready, 1)
            for t in range(T):
                last = pe.matmul(ps[0:J, 512 * 3 + P * t:512 * 3 + P * (t + 1)], kvs[:, t, :], vw[:, t % CT, :], start=True, stop=True)
            last.then_inc(v_ready, 1)
            pe.wait_ge(k_saved, 1)
            pe.wait_ge(q_copied, T)
            for g in range(G):
                t, h = g // HP, g % HP
                if g >= 4:
                    pe.wait_ge(qk_saved, g - 3)
                for i in range(NK):
                    last = pe.matmul(bank(4 + g % 4)[:, J * i:J * (i + 1)], XN[D * h:D * (h + 1), t, P * i:P * (i + 1)],
                                     ks[D * h:D * (h + 1), t, :], start=True, stop=True)
                last.then_inc(qk_ready, 1)

            def layer1(s, g):
                c, q, hf = s // 8, s % 8 // 2, s % 2
                if s % 8 == 0:
                    pe.wait_ge(mv_ready, CHUNKS * g + c + 1)
                pe.matmul(bank(s % 2), wl1[32 * q:32 * q + 4 * NR, :], mv[c % 2][32 * q:32 * q + 4 * NR, HALF * hf:HALF * (hf + 1)],
                          start=True, stop=True).then_inc(z1_ready, 1)

            def layer3(s, g):
                c, q, hf = s // 8, s % 8 // 2, s % 2
                pe.wait_ge(h2_ready, STEPS * g + s + 1)
                for i in range(4):
                    a = J * (4 * hf + i) + 8 * q + c
                    last = pe.matmul(bank(4)[:, a:a + 33:32], h2[s % 2][:, P * i:P * (i + 1)], w3bd[:, :], start=True, stop=True)
                return last

            pe.wait_ge(w1_in, 16 * 4 * NR)
            pe.wait_ge(qk_saved, G)
            layer1(0, 0)
            layer1(1, 0)
            with pe.Fori(0, G) as g:
                for s in range(STEPS):
                    pe.wait_ge(h1_ready, STEPS * g + s + 1)
                    pe.matmul(bank(2 + s % 2), w2bd[:, :], h1[s % 4], start=True, stop=True).then_inc(z2_ready, 1)
                    layer1(s + 2, g)
                    if s == 1:
                        pe.wait_ge(bias_saved, g + 1)
                    if s >= 1:
                        layer3(s - 1, g)
                layer3(STEPS - 1, g).then_inc(bias_ready, 1)

            for g in range(G):
                t, h = g // HP, g % HP
                pe.wait_ge(normed, t + 1)
                if g == 0:
                    pe.wait_ge(h1_ready, STEPS * G + 2)
                if g >= 2:
                    pe.wait_ge(aT_saved, g - 1)
                for i in range(NK):
                    last = pe.transpose(ps[0:J, 1024 * (g % 2) + P * i:1024 * (g % 2) + P * (i + 1)],
                                        SIM[:, g, J * i:J * (i + 1)], ident[:, :])
                last.then_inc(aT_ready, 1)
                pe.wait_ge(aT_saved, g + 1)
                if h == 0 and t >= 2:
                    pe.wait_ge(o_saved, t - 1)
                for hf in range(2):
                    a = 512 * (4 + 2 * (t % 2) + hf)
                    last = pe.matmul(ps[D * h:D * (h + 1), a:a + HALF], vs[:, t, D * h:D * (h + 1)],
                                     att[g % 2][:, HALF * hf:HALF * (hf + 1)], start=True, stop=True)
                if h == HP - 1:
                    last.then_inc(o_ready, 1)
            pe.wait_ge(ld_late, 16 * 6)
            pe.wait_ge(o_saved, T)
            for n in range(T):
                b, hf = n // 2, n % 2
                for ct in range(CT):
                    r = CT * n + ct
                    if r >= 4:
                        pe.wait_ge(x1_ready, r - 3)
                    for kt in range(CT):
                        last = pe.matmul(bank(r % 4), outw[:, kt, P * ct:P * (ct + 1)], ao[:, CT * b + kt, HALF * hf:HALF * (hf + 1)],
                                         start=(kt == 0), stop=(kt == CT - 1))
                    last.then_inc(y_ready, 1)
            pe.wait_ge(x1_ready, 2 * T)
            for n in range(T):
                b, hf = n // 2, n % 2
                pe.wait_ge(xn2_ready, CT * (n + 1))
                for f in range(FT):
                    r = FT * n + f
                    if r >= 4:
                        pe.wait_ge(hid_saved, r - 3)
                    for kt in range(CT):
                        last = pe.matmul(bank(f % 4), m1[:, kt, P * f:P * (f + 1)], XN[:, CT * b + kt, HALF * hf:HALF * (hf + 1)],
                                         start=(kt == 0), stop=(kt == CT - 1))
                    last.then_inc(hid_ready, 1)
                pe.wait_ge(hid_saved, FT * (n + 1))
                for ct in range(CT):
                    r = CT * n + ct
                    if r >= 4:
                        pe.wait_ge(x2_ready, r - 3)
                    for f in range(FT):
                        last = pe.matmul(bank(4 + r % 4), m2[:, f, P * ct:P * (ct + 1)], hm[:, f, :],
                                         start=(f == 0), stop=(f == FT - 1))
                    last.then_inc(m_ready, 1)

            pe.wait_ge(x2_ready, 2 * T)
            wv = wqkv[:, :, :].rearrange("p t (k n) -> p t k n", k=3)
            for n in range(2 * NK):
                b, jt = n // NK, n % NK
                if n >= 4:
                    pe.wait_ge(vv_saved, n - 3)
                for kt in range(CT):
                    last = pe.matmul(bank(4 + n % 4)[:, 0:C], X[:, CT * b + kt, P * jt:P * (jt + 1)], wv[:, kt, 2, :],
                                     start=(kt == 0), stop=(kt == CT - 1))
                last.then_inc(vv_ready, 1)
            for n in range(2 * T):
                which, t = n // T, n % T
                b, mt = t // CT, t % CT
                if n >= 2:
                    pe.wait_ge(f_ready, n - 1)
                for hf in range(2):
                    for kt in range(CT):
                        last = pe.matmul(bank(2 * (n % 2) + hf), wv[:, kt, which, P * mt:P * (mt + 1)],
                                         X[:, CT * b + kt, HALF * hf:HALF * (hf + 1)], start=(kt == 0), stop=(kt == CT - 1))
                last.then_inc(p_ready, 1)

            def scores(u):
                i, it = u // NK, u % NK
                for jh in range(2):
                    for st in range(2):
                        last = pe.matmul(bank(2 * (u % 2) + jh), QS[i][st][:, P * it:P * (it + 1)],
                                         KS[i][st][:, HALF * jh:HALF * (jh + 1)], start=(st == 0), stop=(st == 1))
                last.then_inc(sc_ready, 1)

            def weigh(u, k):
                pe.wait_ge(pTa_saved, 16 * k + u + 1)
                pe.wait_ge(pTd_saved, 16 * k + u + 1)
                pe.wait_ge(oo_saved, 16 * k + max(u - 1, 0) + 1)
                for jt in range(NK):
                    last = pe.matmul(bank(6 + u % 2)[:, 0:D], PTS[u % 2][:, P * jt:P * (jt + 1)], V[:, jt, 2 * k + u // NK, :],
                                     start=(jt == 0), stop=(jt == NK - 1))
                last.then_inc(oo_ready, 1)

            pe.wait_ge(vv_saved, 2 * NK)
            pe.wait_ge(f_ready, 2 * T)
            with pe.Fori(0, G // 2) as k:
                pe.wait_ge(st_in[0], 256 * k + 256)
                scores(0)
                for u in range(16):
                    if u + 1 == NK:
                        pe.wait_ge(st_in[1], 256 * k + 256)
                    if u + 1 < 16:
                        if u >= 1:
                            pe.wait_ge(pr_ready, 16 * k + u)
                        scores(u + 1)
                    if u >= 1:
                        weigh(u - 1, k)
                    pe.wait_ge(pr_ready, 16 * k + u + 1)
                    for jt in range(NK):
                        last = pe.transpose(bank(4, 2)[:, P * jt:P * (jt + 1)], PR[u % 2][:, P * jt:P * (jt + 1)], ident[:, :])
                    last.then_inc(pT_ready, 1)
                weigh(15, k)
            pe.wait_ge(oo_saved, 16 * (G // 2) + 1)
            for n in range(2 * T):
                t, hf = n // 2, n % 2
                b, ct = t // CT, t % CT
                if n >= 4:
                    pe.wait_ge(rT_saved, n - 3)
                for i in range(4):
                    last = pe.transpose(bank(n % 4)[:, P * i:P * (i + 1)],
                                        RES[:, 4 * hf + i, NH * b + HP * ct:NH * b + HP * (ct + 1), :].rearrange("p n d -> p (n d)"),
                                        ident[:, :])
                last.then_inc(rT_ready, 1)
            for n in range(2 * T):
                b, ct, hf = n // 4, n // 2 % 2, n % 2
                pe.wait_ge(rT_saved, 4 * b + 4)
                if n >= 4:
                    pe.wait_ge(fin_saved, n - 3)
                for kt in range(CT):
                    last = pe.matmul(bank(4 + n % 4), wout[:, kt, P * ct:P * (ct + 1)], rT[:, CT * b + kt, HALF * hf:HALF * (hf + 1)],
                                     start=(kt == 0), stop=(kt == CT - 1))
                last.then_inc(fin_ready, 1)


def kernel(**inputs):
    import numpy as _np
    import concourse.bacc as _bacc
    from concourse import mybir as _mybir
    from concourse.bass_utils import run_bass_kernel_spmd as _run

    a = {k: _np.asarray(v) for k, v in inputs.items()}
    L0, L1 = "L0_conv_", "L1_conv_"

    def col(x):
        return x.reshape(-1, P).T

    def rep(x, n):
        return _np.tile(x, (n, 1))

    bqkv = a[L1 + "b_qkv"].reshape(NH, 3, D)
    part = _np.arange(P)
    vecs = _np.concatenate([
        col(a[L0 + "bn1_g"]), col(a[L0 + "bn1_b"]), col(a[L0 + "bn2_g"]), col(a[L0 + "bn2_b"]), col(a[L0 + "out_b"]),
        col(a[L0 + "mlp_b2"]), col(a[L1 + "b_out"]), col(a[L0 + "mlp_b1"]),
        rep(a[L0 + "off_dw_w"].reshape(D, TAPS * TAPS), HP), rep(a[L0 + "off_dw_b"].reshape(D, 1), HP),
        rep(a[L0 + "cpb_b1"].reshape(CH, 1), 2), rep(a[L0 + "cpb_b2"].reshape(CH, 1), 2), rep(a[L0 + "cpb_b3"].reshape(1, 1), P),
        rep(a[L0 + "off_pw_w"].T, HP), col(bqkv[:, 0].reshape(-1)), col(bqkv[:, 1].reshape(-1)),
        (part % W).reshape(P, 1).astype(_np.float32),
        (4 * _np.arange(NK)[None, :] + (part // W)[:, None]).astype(_np.float32)], axis=1)
    j = _np.arange(J)
    gq = (2.0 * _np.arange(W, dtype=_np.float32) / _np.float32(W - 1) - 1.0).astype(_np.float32)
    arrays = {
        "x": a["x"].reshape(B, C, N), "vecs": vecs, "ident": _np.eye(P, dtype=_np.float32),
        "gridj": _np.concatenate([_np.tile(j % KD, (G, 1)), _np.tile(j // KD, (G, 1))]).astype(_np.float32),
        "gridq": _np.tile(gq, (2 * G, 1)),
        "qwT": a[L0 + "qw"].transpose(0, 2, 1), "kwT": a[L0 + "kw"].transpose(0, 2, 1), "vwT": a[L0 + "vw"].transpose(0, 2, 1),
        "cw1": a[L0 + "cpb_w1"], "cw2": a[L0 + "cpb_w2"], "cw3": a[L0 + "cpb_w3"],
        "out_wT": a[L0 + "out_w"].T, "m1T": a[L0 + "mlp_w1"].T, "m2T": a[L0 + "mlp_w2"].T,
        "wqkv": a[L1 + "W_qkv"].reshape(C, NH, 3, D).transpose(0, 2, 1, 3).reshape(C, 3 * C), "wout": a[L1 + "W_out"], "bv": bqkv[:, 2],
    }
    arrays = {k: _np.ascontiguousarray(v) for k, v in arrays.items()}
    nc = _bacc.Bacc("TRN2", target_bir_lowering=False, num_devices=1)
    d = {k: nc.dram_tensor("in_" + k, v.shape, _mybir.dt.from_np(v.dtype), kind="ExternalInput").ap() for k, v in arrays.items()}
    out = nc.dram_tensor("out", (B, C, N), _mybir.dt.float32, kind="ExternalOutput").ap()
    build(nc, d, out)
    r = _run(nc, [{"in_" + k: v for k, v in arrays.items()}], core_ids=[0])
    return _np.asarray(r.results[0]["out"]).reshape(B, C, H, W)
```

```python
import concourse.bass as bass
from concourse import mybir
from contextlib import ExitStack
import numpy as np

P = 128
B, C, H, W = 2, 256, 32, 32
N = H * W
CT = C // P
T = B * CT
NH, D = 8, 32
G = B * NH
HP = P // D
KD = 8
J = KD * KD
FT = 4 * C // P
TAPS, STRIDE = 6, 4
PADW, PADR = W + 2, 36
CH = 64
HALF = N // 2
NK = N // P
BN_INV = 1.0 / float(np.sqrt(np.float32(1.0 + 1e-5)))
SCALE = D ** -0.5

CHUNKS, STEPS = 8, 64
PARTS_S = [0, 0, 1, 1, 0, 2]
PARTS_W = [0, 1, 0, 1, 2, 0]
NR = len(PARTS_S)
ROWS = 4 * NR + 3
AHEAD1, AHEAD2 = 5, 3
RING = 4
LOG_MAX = 1.5

Q_STACK = [[0, 0, 1, 1], [0, 2, 1, 2]]
K_STACK = [[0, 1, 0, 1], [2, 0, 2, 1]]

VEC = {}
_at = 0
for _n, _w in [("bn1_g", 2), ("bn1_b", 2), ("bn2_g", 2), ("bn2_b", 2), ("out_b", 2), ("mlp_b2", 2), ("b_out", 2),
               ("mlp_b1", 8), ("dw_w", 36), ("dw_b", 1), ("cb1", 1), ("cb2", 1), ("cw1T", 2), ("cw3", 1), ("one_rows", 1), ("cb3", 1), ("pw", 2),
               ("bq", 2), ("bk", 2), ("px", 1), ("py", 8)]:
    VEC[_n] = (_at, _w)
    _at += _w
NVEC = _at


def build(nc, d, out):
    fp32, bf16, fp16, fp32r = mybir.dt.float32, mybir.dt.bfloat16, mybir.dt.float16, mybir.dt.float32r
    i32 = mybir.dt.int32
    ALU, ACT, AX = mybir.AluOpType, mybir.ActivationFunctionType, mybir.AxisListType

    ctx = ExitStack()
    with ctx:
        def sb(name, shape, dt=fp32):
            return ctx.enter_context(nc.sbuf_tensor(name, shape, dt))

        def sem(name):
            return ctx.enter_context(nc.semaphore(name))

        def dram(name, shape, dt):
            return nc.dram_tensor(name, shape, dt, kind="Internal").ap()

        grid_d = dram("grid_d", [2 * G, J], fp32)
        s_d = dram("s_d", [3, 2, G, J * W], bf16)
        w1_d = dram("w1_d", [3, 3, CH], bf16)
        q_d = dram("q_d", [3, G * D, N], bf16)
        k_d = dram("k_d", [3, G * D, N], bf16)

        vec = sb("vec", [P, NVEC])
        ident = sb("ident", [P, P])
        gridj = sb("gridj", [2 * G, J])
        gridq = sb("gridq", [2 * G, W])
        X = sb("X", [P, T, N])
        XN = sb("XN", [P, T, N])
        qpad = sb("qpad", [P, T * PADR + 4, PADW])
        qw = sb("qw", [P, CT, P])
        kw = sb("kw", [P, CT, P])
        vw = sb("vw", [P, CT, P])
        outw = sb("outw", [P, CT, C])
        m1 = sb("m1", [P, CT, 4 * C])
        m2 = sb("m2", [P, FT, C])
        late = qpad[:, :, :].rearrange("p a b -> p (a b)")
        wqkv = late[:, 0:CT * 3 * C].rearrange("p (t n) -> p t n", t=CT)
        wout = late[:, CT * 3 * C:CT * 4 * C].rearrange("p (t n) -> p t n", t=CT)
        bv = sb("bv", [P, NH, D])
        sc = sb("sc", [P, 4])
        conv = sb("conv", [P, T * 9, KD])
        gel = sb("gel", [P, T * 9, KD])
        pwl = sb("pwl", [P, T, 2, G])
        off = sb("off", [2 * G, J])
        vpos = sb("vpos", [2 * G, J])
        npos = sb("npos", [2 * G, J])
        gxy = sb("gxy", [2 * G, J])
        w1s = sb("w1s", [3, CH])
        w1r = sb("w1r", [3, CH])
        w1p = sb("w1p", [3, 3, CH], bf16)
        wl1 = sb("wl1", [P, P], bf16)
        w2bd = sb("w2bd", [P, P])
        w2T = sb("w2T", [P, P])
        w2h, w2l = sb("w2h", [P, P], fp32r), sb("w2l", [P, P], fp32r)
        w3s = sb("w3s", [P, 2], bf16)
        cs = sb("cs", [P, 12])
        sx = sb("sx", [P, G + 1, CHUNKS, W], bf16)
        sy = sb("sy", [P, G + 1, CHUNKS, W], bf16)
        SIM = sb("SIM", [P, G, NK * J])
        big = sb("big", [P, 12, N])
        kvs = sb("kvs", [P, T, J])
        ks = sb("ks", [P, T, J])
        vs = sb("vs", [J, T, P])
        mv = [sb(f"mv{i}", [P, N], bf16) for i in range(2)]
        gb = m1[:, :, :]
        hx = m2[:, 0:4, :].rearrange("p a b -> p (a b)")
        h1h, h1l = sb("h1h", [P, RING, HALF], fp32r), sb("h1l", [P, RING, HALF], fp32r)
        h2 = [big[:, i // 2, HALF * (i % 2):HALF * (i % 2 + 1)] for i in range(RING)]
        h2h = [big[:, 2, 256 * i:256 * (i + 1)].bitcast(fp16) for i in range(RING)]
        h2l = [big[:, 3, 256 * i:256 * (i + 1)].bitcast(fp16) for i in range(RING)]
        smax = sb("smax", [P, HP * NK])
        ssum = sb("ssum", [P, HP * NK])
        srec = sb("srec", [P, HP * NK])

        pos = SIM[0:2 * G, 0:4, :].rearrange("p a b -> p (a b)")
        pp = SIM[0:2 * G, 4:8, :].rearrange("p a b -> p (a b)")
        pn = SIM[0:2 * G, 8:12, :].rearrange("p a b -> p (a b)")
        s3 = SIM[0:2 * G, 12:16, :].rearrange("p a b -> p (a b)")
        xnT = big[:, 0:4, :]
        wsm = big[:, 4:12, :]
        att = [big[0:J, i, :] for i in (0, 1)]
        ao = big[:, 2:6, :]
        hm = big[:, 6:10, :].rearrange("p a b -> p (a b)").rearrange("p (f n) -> p f n", f=FT)
        spt = [gb[0:2 * G, 0, :].bitcast(bf16), gb[0:2 * G, 1, :].bitcast(bf16), m2[0:2 * G, 0:4, :].rearrange("p a b -> p (a b)").bitcast(bf16)]

        ps = ctx.enter_context(nc.psum_tensor("ps", [P, 8 * 512], fp32))

        def bank(i, n=1):
            return ps[:, 512 * i:512 * (i + n)]

        def v(name, i=0, n=1):
            a = VEC[name][0] + i
            return vec[:, a:a + n]

        ld_vec, ld_bd, ld_w1, ld_late = (sem(x) for x in ("ld_vec", "ld_bd", "ld_w1", "ld_late"))
        ld_x = [sem(f"ld_x{b}") for b in range(B)]
        cleared = sem("cleared")
        dve_chain = sem("dve_chain")
        scales_ready, xn_ready, q_ready, q_saved = (sem(x) for x in ("scales_ready", "xn_ready", "q_ready", "q_saved"))
        xT_ready, xT_saved, conv_ready, gelu_ready = (sem(x) for x in ("xT_ready", "xT_saved", "conv_ready", "gelu_ready"))
        pwl_ready, pw_ready, off_ready, gxy_ready = (sem(x) for x in ("pwl_ready", "pw_ready", "off_ready", "gxy_ready"))
        grid_out, grid_in, w1p_ready, w1_out, w1_in = (sem(x) for x in ("grid_out", "grid_in", "w1p_ready", "w1_out", "w1_in"))
        pn_ready, ln_ready, sparts_ready, s_out, s_in = (sem(x) for x in ("pn_ready", "ln_ready", "sparts_ready", "s_out", "s_in"))
        ws_ready, kv_ready, kv_saved, k_ready, v_ready, k_saved, v_saved = (
            sem(x) for x in ("ws_ready", "kv_ready", "kv_saved", "k_ready", "v_ready", "k_saved", "v_saved"))
        abs_ready, hat_ready = sem("abs_ready"), sem("hat_ready")
        q_copied, qk_ready, qk_saved = sem("q_copied"), sem("qk_ready"), sem("qk_saved")
        mv_ready, z1_ready, h1h_ready, h1l_ready, z2_ready, h2_ready, h2h_ready = (
            sem(x) for x in ("mv_ready", "z1_ready", "h1h_ready", "h1l_ready", "z2_ready", "h2_ready", "h2h_ready"))
        h2l_pool, h2l_dve, bias_ready, bias_saved = (sem(x) for x in ("h2l_pool", "h2l_dve", "bias_ready", "bias_saved"))
        bound_in, bound_ready, w2s_ready, w2sT_ready, w2_ready = (
            sem(x) for x in ("bound_in", "bound_ready", "w2s_ready", "w2sT_ready", "w2_ready"))
        shifted, exped, normed, aT_ready, aT_saved, o_ready, o_saved = (
            sem(x) for x in ("shifted", "exped", "normed", "aT_ready", "aT_saved", "o_ready", "o_saved"))
        y_ready, x1_ready, xn2_ready, hid_ready, hid_saved, m_ready, x2_ready = (
            sem(x) for x in ("y_ready", "x1_ready", "xn2_ready", "hid_ready", "hid_saved", "m_ready", "x2_ready"))
        p_ready, f_ready, f_hi, f_res, f_mid, f_lo = (
            sem(x) for x in ("p_ready", "f_ready", "f_hi", "f_res", "f_mid", "f_lo"))
        parts_out = [sem("parts_out0"), sem("parts_out1")]
        max_done, rec_done = sem("max_done"), sem("rec_done")
        vv_ready, vv_saved = sem("vv_ready"), sem("vv_saved")
        st_in = [sem("st_in0"), sem("st_in1")]
        sc_ready, mx_ready, pr_ready, pT_ready, pTa_saved, pTd_saved, oo_ready, oo_saved = (
            sem(x) for x in ("sc_ready", "mx_ready", "pr_ready", "pT_ready", "pTa_saved", "pTd_saved", "oo_ready", "oo_saved"))
        rT_ready, rT_saved, fin_ready, fin_saved, stored = (
            sem(x) for x in ("rT_ready", "rT_saved", "fin_ready", "fin_saved", "stored"))

        V = big[:, 0:4, :].rearrange("p a b -> p (a b)").rearrange("p (j n d) -> p j n d", j=NK, n=G)
        RES = big[:, 4:8, :].rearrange("p a b -> p (a b)").rearrange("p (i n d) -> p i n d", i=NK, n=G)
        rT = XN
        PR = [big[:, 8, :], big[:, 9, :]]
        PTS = [big[:, 10, :], big[:, 11, :]]
        F = [SIM[:, 0:2, :].rearrange("p a b -> p (a b)"), SIM[:, 2:4, :].rearrange("p a b -> p (a b)")]
        R = [SIM[:, 4:6, :].rearrange("p a b -> p (a b)"), SIM[:, 6:8, :].rearrange("p a b -> p (a b)")]
        part = [[SIM[:, 8 + 3 * i + a, :].bitcast(bf16) for a in range(3)] for i in range(2)]
        QS = [[SIM[:, 4 * i + a, :].bitcast(bf16) for a in range(2)] for i in range(2)]
        KS = [[SIM[:, 4 * i + 2 + a, :].bitcast(bf16) for a in range(2)] for i in range(2)]
        amax = [sb(f"amax{i}", [P, 1]) for i in range(2)]
        aneg = [sb(f"aneg{i}", [P, 1]) for i in range(2)]
        asum = [sb(f"asum{i}", [P, 1]) for i in range(4)]
        arec = [sb(f"arec{i}", [P, 1]) for i in range(2)]

        out_v = out.rearrange("b (c p) n -> p b c n", p=P)
        x_v = d["x"].rearrange("b (c p) n -> p b c n", p=P)

        block = ctx.enter_context(nc.Block())

        @block.sync
        def _(sp):
            sp.dma_start(vec[:, :], d["vecs"]).then_inc(ld_vec, 16)
            for b in range(B):
                sp.dma_start(X[:, CT * b:CT * (b + 1), :], x_v[:, b]).then_inc(ld_x[b], 16)
            sp.dma_start(ident[:, :], d["ident"]).then_inc(ld_vec, 16)
            sp.dma_start(gridj[:, :], d["gridj"]).then_inc(ld_vec, 16)
            sp.dma_start(gridq[:, :], d["gridq"]).then_inc(ld_vec, 16)
            sp.wait_ge(cleared, 6)
            for w, src in ((qw, "qwT"), (kw, "kwT"), (vw, "vwT")):
                for h in range(HP):
                    sp.dma_start(w[D * h:D * (h + 1), :, D * h:D * (h + 1)],
                                 d[src].rearrange("(t h) c o -> h c t o", h=HP)[h]).then_inc(ld_bd, 16)
            for h in range(2):
                sp.dma_start(w2bd[CH * h:CH * (h + 1), CH * h:CH * (h + 1)], d["cw2"]).then_inc(ld_bd, 16)
                sp.dma_start(w2T[CH * h:CH * (h + 1), CH * h:CH * (h + 1)], d["cw2T"]).then_inc(ld_bd, 16)
            sp.wait_ge(w1p_ready, 1)
            sp.dma_start(w1_d, w1p[:, :, :]).then_inc(w1_out, 16)
            sp.wait_ge(w1_out, 16)
            for jh in range(2):
                for c in range(2):
                    for r in range(NR):
                        row = 2 * NR * jh + NR * c + r
                        sp.dma_start(wl1[row:row + 97:32, CH * jh:CH * (jh + 1)],
                                     w1_d[c, PARTS_W[r]:PARTS_W[r] + 1, :].to_broadcast((4, CH))).then_inc(w1_in, 16)
                for a in range(3):
                    sp.dma_start(wl1[4 * NR + a:4 * NR + a + 97:32, CH * jh:CH * (jh + 1)],
                                 w1_d[2, a:a + 1, :].to_broadcast((4, CH))).then_inc(w1_in, 16)
            sp.wait_ge(gxy_ready, 1)
            sp.dma_start(grid_d, gxy[:, :]).then_inc(grid_out, 16)
            sp.wait_ge(sparts_ready, 3)
            for a in range(3):
                sp.dma_start(s_d[a].rearrange("c g n -> (c g) n"), spt[a]).then_inc(s_out, 16)
            sp.wait_ge(s_out, 48)
            sp.wait_ge(cleared, 9 + G + 1)
            sv = s_d.rearrange("a c g (h q n) -> a c h q g n", h=2, q=4)
            for jh in range(2):
                for c in range(2):
                    for r in range(NR):
                        row = 2 * NR * jh + NR * c + r
                        dst = (sx, sy)[c]
                        sp.dma_start(dst[row:row + 97:32, 0:G, :, :].rearrange("p g a b -> p g (a b)"),
                                     sv[PARTS_S[r], c, jh]).then_inc(s_in, 16)
            sp.wait_ge(grid_out, 16)
            sp.dma_start(gb[:, :, :].rearrange("p a b -> p (a b)"),
                         grid_d.rearrange("a b -> (a b)").partition_broadcast(P)).then_inc(grid_in, 16)
            sp.wait_ge(ws_ready, NK)
            sp.wait_ge(q_copied, T)
            for dst, src, n in ((outw, "out_wT", CT), (m1, "m1T", CT), (m2, "m2T", FT), (wqkv, "wqkv", CT), (wout, "wout", CT)):
                sp.dma_start(dst[:, :, :], d[src].rearrange("(t p) n -> p t n", p=P)).then_inc(ld_late, 16)
            sp.dma_start(bv[:, :, :], d["bv"].partition_broadcast(P)).then_inc(ld_late, 16)

            for n in range(2 * T):
                which, t = n // T, n % T
                dst = (q_d, k_d)[which]
                for a, s in enumerate((f_hi, f_mid, f_lo)):
                    sp.wait_ge(s, n + 1)
                    sp.dma_start(dst[a, P * t:P * (t + 1), :], part[n % 2][a]).then_inc(parts_out[n % 2], 16)

            def load_head(i, n):
                for st in range(2):
                    for r in range(HP):
                        sp.dma_start(QS[i][st][D * r:D * (r + 1), :],
                                     q_d[Q_STACK[st][r], bass.ds(n * D, D), :]).then_inc(st_in[i], 16)
                        sp.dma_start(KS[i][st][D * r:D * (r + 1), :],
                                     k_d[K_STACK[st][r], bass.ds(n * D, D), :]).then_inc(st_in[i], 16)

            for i in range(2):
                sp.wait_ge(parts_out[i], 48 * T)
            load_head(0, 0)
            load_head(1, 1)
            with sp.Fori(0, G // 2 - 1) as k:
                sp.wait_ge(sc_ready, 16 * k + 8)
                load_head(0, 2 * k + 2)
                sp.wait_ge(sc_ready, 16 * k + 16)
                load_head(1, 2 * k + 3)

            for n in range(T):
                for hf in range(2):
                    sp.wait_ge(fin_saved, 2 * n + hf + 1)
                    sp.dma_start(out_v[:, n // CT, n % CT, HALF * hf:HALF * (hf + 1)],
                                 X[:, n, HALF * hf:HALF * (hf + 1)]).then_inc(stored, 16)
            sp.wait_ge(stored, 16 * 2 * T)

        @block.gpsimd
        def _(pool):
            for m in (qw[:, :, :], kw[:, :, :], vw[:, :, :], w2T[:, :], w2bd[:, :], wl1[:, :],
                      qpad[:, :, :], pwl[:, :, :, :], sy[:, :, :, :]):
                pool.memset(m, 0.0).then_inc(cleared, 1)
            pool.wait_ge(ld_vec, 64)
            for g in range(G + 1):
                pool.tensor_copy(sx[:, g, :, :], v("one_rows").unsqueeze(2).to_broadcast((P, CHUNKS, W))).then_inc(cleared, 1)

            def spread(i, g, jj):
                shape = (P, H, W)
                pool.tensor_tensor(mv[i][:, :].rearrange("p (a b) -> p a b", a=H),
                                   sx[:, g, jj, :].unsqueeze(1).to_broadcast(shape),
                                   sy[:, g, jj, :].unsqueeze(2).to_broadcast(shape), ALU.add).then_inc(mv_ready, 1)

            pool.wait_ge(q_saved, 2 * T)
            pool.wait_ge(xT_ready, 2 * T)
            for t in range(T):
                row = PADR * t + 1
                pool.tensor_copy(XN[:, t, :].rearrange("p (a b) -> p a b", b=W), qpad[:, row:row + H, 1:1 + W]).then_inc(q_copied, 1)

            pool.wait_ge(s_in, 16 * 4 * NR)
            def low2(m):
                if m % RING != RING - 1:
                    pool.tensor_tensor(h2l[m % RING], h2[m % RING], h2h[m % RING], ALU.subtract).then_inc(h2l_pool, 1)

            spread(0, 0, 0)
            spread(1, 0, 1)
            for m in range(AHEAD2):
                pool.wait_ge(h2h_ready, m + 1)
                low2(m)
            with pool.Fori(0, G) as g:
                for m in range(AHEAD2, STEPS + AHEAD2):
                    if m % RING != RING - 1:
                        pool.wait_ge(h2h_ready, STEPS * g + m + 1)
                        low2(m)
                    if m % 8 == 0:
                        c = m // 8 + 1
                        pool.wait_ge(z1_ready, STEPS * g + 8 * (c - 1))
                        spread(c % 2, g + c // CHUNKS, c % CHUNKS)

        @block.scalar
        def _(act):
            act.dma_start(w1s[:, :], d["cw1"]).then_inc(ld_w1, 16)
            act.wait_ge(scales_ready, 1)
            for t in range(T):
                act.wait_ge(ld_x[t // CT], 16)
                act.activation(XN[:, t, :], X[:, t, :], ACT.Identity, scale=sc[:, t % CT:t % CT + 1],
                               bias=v("bn1_b", t % CT)).then_inc(xn_ready, 1)
            for r in range(2 * T):
                act.wait_ge(xT_ready, r + 1)
                act.activation(xnT[:, r // 2, HALF * (r % 2):HALF * (r % 2 + 1)], bank(r), ACT.Identity).then_inc(xT_saved, 1)
            act.wait_ge(conv_ready, 1)
            act.activation(gel[:, :, :], conv[:, :, :], ACT.Gelu, bias=v("dw_b")).then_inc(gelu_ready, 1)
            act.wait_ge(pw_ready, 1)
            act.activation(off[:, :], ps[0:2 * G, 0:J], ACT.Tanh).then_inc(off_ready, 1)
            act.wait_ge(pn_ready, 1)
            act.activation(pp, pp, ACT.Ln, bias=1.0).then_inc(ln_ready, 1)
            act.wait_ge(pn_ready, 2)
            act.activation(pn, pn, ACT.Ln, bias=1.0).then_inc(ln_ready, 1)
            act.wait_ge(grid_in, 16)
            for i in range(NK + 1):
                dst, src, pixel = (hx[:, :], gb[:, 0, :], v("px")) if i == 0 else (wsm[:, i - 1, :], gb[:, 1, :], v("py", i - 1))
                act.activation(dst, src, ACT.Abs, scale=-1.0, bias=pixel).then_inc(abs_ready, 1)
                act.wait_ge(abs_ready, i + 1)
                act.activation(dst, dst, ACT.Relu, scale=-1.0, bias=1.0).then_inc(hat_ready, 1)
            act.wait_ge(kv_ready, 1)
            act.activation(kvs[:, :, :], bank(1)[:, 0:T * J].rearrange("p (t j) -> p t j", t=T), ACT.Identity).then_inc(kv_saved, 1)
            act.wait_ge(k_ready, 1)
            act.activation(ks[:, :, :], bank(2)[:, 0:T * J].rearrange("p (t j) -> p t j", t=T), ACT.Identity,
                           scale=SCALE).then_inc(k_saved, 1)
            act.wait_ge(v_ready, 1)
            act.activation(vs[:, :, :], ps[0:J, 512 * 3:512 * 4].rearrange("p (t o) -> p t o", t=T), ACT.Identity).then_inc(v_saved, 1)
            act.wait_ge(s_out, 48)
            for g in range(G):
                act.wait_ge(qk_ready, g + 1)
                act.activation(SIM[:, g, :], bank(4 + g % 4), ACT.Identity).then_inc(qk_saved, 1)

            def high1(m):
                act.activation(h1h[:, m % RING, :], bank(m % 2), ACT.Relu).then_inc(h1h_ready, 1)

            def relu2(m):
                act.activation(h2[m % RING], bank(2 + m % 2), ACT.Relu, bias=cs[:, 9:10]).then_inc(h2_ready, 1)

            for m in range(2):
                act.wait_ge(z1_ready, m + 1)
                high1(m)
            act.wait_ge(w2_ready, 1)
            for m in range(AHEAD2):
                act.wait_ge(z2_ready, m + 1)
                relu2(m)
                act.wait_ge(z1_ready, m + 3)
                high1(m + 2)
            with act.Fori(0, G) as g:
                for m in range(AHEAD2, STEPS + AHEAD2):
                    act.wait_ge(z2_ready, STEPS * g + m + 1)
                    relu2(m)
                    act.wait_ge(z1_ready, STEPS * g + m + 3)
                    high1(m + 2)

            for t in range(T):
                act.wait_ge(shifted, t + 1)
                act.activation(SIM[:, HP * t:HP * (t + 1), :], SIM[:, HP * t:HP * (t + 1), :], ACT.Exp).then_inc(exped, 1)
            for g in range(G):
                act.wait_ge(aT_ready, g + 1)
                act.activation(att[g % 2], ps[0:J, 1024 * (g % 2):1024 * (g % 2) + N], ACT.Identity).then_inc(aT_saved, 1)
                if g % HP == HP - 1:
                    t = g // HP
                    act.wait_ge(o_ready, t + 1)
                    act.activation(ao[:, t, :], bank(4 + 2 * (t % 2), 2), ACT.Identity).then_inc(o_saved, 1)
            for n in range(T):
                for ct in range(CT):
                    b, hf = n // 2, n % 2
                    act.wait_ge(x1_ready, CT * n + ct + 1)
                    act.activation(XN[:, CT * b + ct, HALF * hf:HALF * (hf + 1)], X[:, CT * b + ct, HALF * hf:HALF * (hf + 1)],
                                   ACT.Identity, scale=sc[:, CT + ct:CT + ct + 1], bias=v("bn2_b", ct)).then_inc(xn2_ready, 1)
            for n in range(T):
                for f in range(FT):
                    act.wait_ge(hid_ready, FT * n + f + 1)
                    act.activation(hm[:, f, :], bank(f % 4), ACT.Gelu, bias=v("mlp_b1", f)).then_inc(hid_saved, 1)

            for n in range(2 * T):
                which, t = n // T, n % T
                i = n % 2
                act.wait_ge(p_ready, n + 1)
                if n >= 2:
                    act.wait_ge(f_lo, n - 1)
                    act.wait_ge(parts_out[i], 48 * (n // 2))
                act.activation(F[i], bank(2 * i, 2), ACT.Identity, bias=v(("bq", "bk")[which], t % CT)).then_inc(f_ready, 1)
                act.wait_ge(f_ready, n + 1)
                act.activation(part[i][0], F[i], ACT.Copy).then_inc(f_hi, 1)
                act.wait_ge(f_res, n + 1)
                act.activation(part[i][1], R[i], ACT.Copy).then_inc(f_mid, 1)

            with act.Fori(0, G // 2) as k:
                for u in range(16):
                    act.wait_ge(mx_ready, 16 * k + u + 1)
                    act.activation(PR[u % 2], bank(2 * (u % 2), 2), ACT.Exp, scale=SCALE, bias=aneg[u % 2][:, :],
                                   accum_out=asum[u % 4][:, :]).then_inc(pr_ready, 1)
                    act.wait_ge(pT_ready, 16 * k + u + 1)
                    act.activation(PTS[u % 2][:, 0:HALF], bank(4), ACT.Identity).then_inc(pTa_saved, 1)
            for n in range(2 * T):
                act.wait_ge(rT_ready, n + 1)
                act.activation(rT[:, n // 2, HALF * (n % 2):HALF * (n % 2 + 1)], bank(n % 4), ACT.Identity).then_inc(rT_saved, 1)

        @block.vector
        def _(dve):
            chain = [0]

            def link(ins):
                chain[0] += 1
                ins.then_inc(dve_chain, 1)
                dve.wait_ge(dve_chain, chain[0])

            dve.wait_ge(ld_vec, 64)
            dve.tensor_scalar(sc[:, 0:CT], v("bn1_g", 0, CT), BN_INV, None, ALU.mult).then_inc(scales_ready, 1)
            dve.tensor_scalar(sc[:, CT:2 * CT], v("bn2_g", 0, CT), BN_INV, None, ALU.mult)
            dve.wait_ge(ld_w1, 16)
            link(dve.tensor_copy(w1p[:, 0, :], w1s[:, :]))
            link(dve.tensor_tensor(w1r[:, :], w1s[:, :], w1p[:, 0, :], ALU.subtract))
            link(dve.tensor_copy(w1p[:, 1, :], w1r[:, :]))
            dve.tensor_tensor(w1p[:, 2, :], w1r[:, :], w1p[:, 1, :], ALU.subtract).then_inc(w1p_ready, 1)
            dve.wait_ge(ld_bd, 16 * (3 * HP + 4))
            link(dve.tensor_scalar(w2h[:, :], w2bd[:, :], -1.0, None, ALU.mult))
            link(dve.tensor_tensor(w2l[:, :], w2bd[:, :], w2h[:, :].bitcast(fp32), ALU.max))
            link(dve.tensor_scalar(cs[:, 0:2], v("cw1T", 0, 2), -1.0, None, ALU.mult))
            link(dve.tensor_tensor(cs[:, 0:2], cs[:, 0:2], v("cw1T", 0, 2), ALU.max))
            link(dve.tensor_tensor(cs[:, 2:3], cs[:, 0:1], cs[:, 1:2], ALU.add))
            link(dve.tensor_scalar(cs[:, 3:4], v("cb1"), -1.0, None, ALU.mult))
            link(dve.tensor_tensor(cs[:, 3:4], cs[:, 3:4], v("cb1"), ALU.max))
            link(dve.scalar_tensor_tensor(cs[:, 4:5], cs[:, 2:3], LOG_MAX, cs[:, 3:4], ALU.mult, ALU.add))
            dve.sem_inc(bound_in, 1)
            link(dve.tensor_scalar(cs[:, 5:6], v("cb2"), -1.0, None, ALU.mult))
            link(dve.tensor_tensor(cs[:, 5:6], cs[:, 5:6], v("cb2"), ALU.max))
            link(dve.tensor_scalar(cs[:, 6:7], v("cw3"), -1.0, None, ALU.mult))
            link(dve.tensor_tensor(cs[:, 6:7], cs[:, 6:7], v("cw3"), ALU.max))
            dve.wait_ge(bound_ready, 1)
            link(dve.tensor_tensor(cs[:, 7:8], bank(0)[:, 0:1], cs[:, 5:6], ALU.add))
            link(dve.tensor_tensor(cs[:, 7:8], cs[:, 7:8], cs[:, 6:7], ALU.mult))
            link(dve.tensor_scalar(cs[:, 7:8], cs[:, 7:8], 2.0 ** -40, None, ALU.max))
            link(dve.tensor_scalar(cs[:, 7:8].bitcast(i32), cs[:, 7:8].bitcast(i32), 0x7F800000, None, ALU.bitwise_and))
            link(dve.reciprocal(cs[:, 8:9], cs[:, 7:8]))
            link(dve.scalar_tensor_tensor(cs[:, 8:9], cs[:, 8:9], 2.0 ** 14, cs[:, 6:7], ALU.mult, ALU.mult))
            link(dve.tensor_tensor(cs[:, 9:10], v("cb2"), cs[:, 8:9], ALU.mult))
            link(dve.tensor_scalar(w2T[:, :], w2T[:, :], cs[:, 8:9], None, ALU.mult))
            dve.sem_inc(w2s_ready, 1)
            dve.wait_ge(cleared, 5)
            link(dve.memset(w3s[:, :], 0.0))
            link(dve.tensor_scalar(cs[:, 10:11], v("cw3"), 0.0, None, ALU.is_gt))
            link(dve.tensor_scalar(cs[:, 11:12], v("cw3"), 0.0, None, ALU.is_lt))
            link(dve.tensor_tensor(cs[:, 10:11], cs[:, 10:11], cs[:, 11:12], ALU.subtract))
            for h in range(2):
                a, b = CH * h, CH * (h + 1)
                link(dve.scalar_tensor_tensor(w3s[a:b, h:h + 1], cs[a:b, 7:8], 2.0 ** -14, cs[a:b, 10:11], ALU.mult, ALU.mult))
            dve.wait_ge(w2sT_ready, 1)
            link(dve.tensor_copy(w2h[:, :], bank(0)[:, 0:P]))
            dve.tensor_tensor(w2l[:, :], bank(0)[:, 0:P], w2h[:, :].bitcast(fp32), ALU.subtract).then_inc(w2_ready, 1)
            dve.wait_ge(cleared, 8)
            for h in range(HP):
                for t in range(T):
                    last = dve.tensor_copy(pwl[D * h:D * (h + 1), t, :, HP * t + h], vec[D * h:D * (h + 1), VEC["pw"][0]:VEC["pw"][0] + 2])
            last.then_inc(pwl_ready, 1)
            for r in range(2 * T):
                t, hf = r // 2, r % 2
                dve.wait_ge(q_ready, r + 1)
                row = PADR * t + 1 + (H // 2) * hf
                dve.tensor_copy(qpad[:, row:row + H // 2, 1:1 + W], bank(r).rearrange("p (a b) -> p a b", b=W)).then_inc(q_saved, 1)
            dve.wait_ge(q_saved, 2 * T)
            for tap in range(TAPS * TAPS):
                ky, kx = tap // TAPS, tap % TAPS
                src = qpad[:, ky:ky + STRIDE * (T * 9 - 1) + 1:STRIDE, kx:kx + STRIDE * (KD - 1) + 1:STRIDE]
                if tap == 0:
                    link(dve.tensor_scalar(conv[:, :, :], src, v("dw_w", 0), None, ALU.mult))
                else:
                    link(dve.scalar_tensor_tensor(conv[:, :, :], src, v("dw_w", tap), conv[:, :, :], ALU.mult, ALU.add))
            dve.sem_inc(conv_ready, 1)
            dve.wait_ge(off_ready, 1)
            link(dve.scalar_tensor_tensor(vpos[:, :], off[:, :], 4.0, gridj[:, :], ALU.mult, ALU.add))
            link(dve.tensor_scalar(npos[:, :], vpos[:, :], 2.0 / (KD - 1), -1.0, ALU.mult, ALU.add))
            link(dve.tensor_scalar(gxy[:, :], npos[:, :], 1.0, W / 2.0, ALU.add, ALU.mult))
            link(dve.tensor_scalar(gxy[:, :], gxy[:, :], -0.5, None, ALU.add))
            dve.sem_inc(gxy_ready, 1)
            shape = (2 * G, J, W)
            r3 = "p (j q) -> p j q"
            link(dve.tensor_tensor(pos.rearrange(r3, j=J), gridq[:, :].unsqueeze(1).to_broadcast(shape),
                                   npos[:, :].unsqueeze(2).to_broadcast(shape), ALU.subtract))
            dve.tensor_scalar(pp, pos, 0.0, None, ALU.max).then_inc(pn_ready, 1)
            dve.tensor_scalar(pn, pos, -1.0, 0.0, ALU.mult, ALU.max).then_inc(pn_ready, 1)
            dve.wait_ge(ln_ready, 2)
            link(dve.tensor_tensor(s3, pp, pn, ALU.subtract))
            link(dve.tensor_copy(spt[0], s3))
            link(dve.tensor_tensor(pos, s3, spt[0], ALU.subtract))
            link(dve.tensor_copy(spt[1], pos))
            dve.tensor_tensor(spt[2], pos, spt[1], ALU.subtract).then_inc(sparts_ready, 3)
            dve.wait_ge(hat_ready, 1)
            for k in range(NK):
                dve.wait_ge(hat_ready, k + 2)
                dve.tensor_tensor(wsm[:, k, :], wsm[:, k, :], hx[:, :], ALU.mult).then_inc(ws_ready, 1)

            def low1(m):
                dve.scalar_tensor_tensor(h1l[:, m % RING, :], bank(m % 2), 0.0, h1h[:, m % RING, :].bitcast(fp32),
                                         ALU.max, ALU.subtract).then_inc(h1l_ready, 1)

            def high2(m):
                dve.tensor_copy(h2h[m % RING], h2[m % RING]).then_inc(h2h_ready, 1)

            dve.wait_ge(qk_saved, G)
            dve.sem_inc(bias_saved, 1)
            for m in range(2):
                dve.wait_ge(h1h_ready, m + 1)
                low1(m)
            for m in range(AHEAD2):
                dve.wait_ge(h2_ready, m + 1)
                high2(m)
                dve.wait_ge(h1h_ready, m + 3)
                low1(m + 2)
            with dve.Fori(0, G) as g:
                for m in range(AHEAD2, STEPS + AHEAD2):
                    dve.wait_ge(h2_ready, STEPS * g + m + 1)
                    high2(m)
                    dve.wait_ge(h1h_ready, STEPS * g + m + 3)
                    low1(m + 2)
                    if m % RING == RING - 1:
                        dve.wait_ge(h2h_ready, STEPS * g + m + 1)
                        dve.tensor_tensor(h2l[m % RING], h2[m % RING], h2h[m % RING], ALU.subtract).then_inc(h2l_dve, 1)
                dve.wait_ge(bias_ready, g + 1)
                dve.tensor_tensor(SIM[:, g, :], bank(4), SIM[:, g, :], ALU.add).then_inc(bias_saved, 1)
            dve.wait_ge(bias_saved, G + 1)

            for t in range(T):
                s = SIM[:, HP * t:HP * (t + 1), :].rearrange("p g (i j) -> p (g i) j", j=J)
                shape = (P, HP * NK, J)
                link(dve.tensor_reduce(smax[:, :], s, AX.X, ALU.max))
                link(dve.tensor_scalar(smax[:, :], smax[:, :], v("cb3"), None, ALU.add))
                dve.scalar_tensor_tensor(s, s, v("cb3"), smax[:, :].unsqueeze(2).to_broadcast(shape),
                                         ALU.add, ALU.subtract).then_inc(shifted, 1)
                dve.wait_ge(exped, t + 1)
                link(dve.tensor_reduce(ssum[:, :], s, AX.X, ALU.add))
                link(dve.reciprocal(srec[:, :], ssum[:, :]))
                dve.tensor_tensor(s, s, srec[:, :].unsqueeze(2).to_broadcast(shape), ALU.mult).then_inc(normed, 1)
            for n in range(T):
                b, hf = n // 2, n % 2
                for ct in range(CT):
                    r = CT * n + ct
                    xs = X[:, CT * b + ct, HALF * hf:HALF * (hf + 1)]
                    dve.wait_ge(y_ready, r + 1)
                    dve.scalar_tensor_tensor(xs, bank(r % 4), v("out_b", ct), xs, ALU.add, ALU.add).then_inc(x1_ready, 1)
            for n in range(T):
                b, hf = n // 2, n % 2
                for ct in range(CT):
                    r = CT * n + ct
                    xs = X[:, CT * b + ct, HALF * hf:HALF * (hf + 1)]
                    dve.wait_ge(m_ready, r + 1)
                    dve.wait_ge(xn2_ready, r + 1)
                    dve.scalar_tensor_tensor(xs, bank(4 + r % 4), v("mlp_b2", ct), xs, ALU.add, ALU.add).then_inc(x2_ready, 1)
            for n in range(2 * NK):
                b, jt = n // NK, n % NK
                dve.wait_ge(vv_ready, n + 1)
                dve.tensor_tensor(V[:, jt, NH * b:NH * (b + 1), :], bank(4 + n % 4)[:, 0:C].rearrange("p (n d) -> p n d", d=D),
                                  bv[:, :, :], ALU.add).then_inc(vv_saved, 1)
            for n in range(2 * T):
                i = n % 2
                dve.wait_ge(f_hi, n + 1)
                dve.tensor_tensor(R[i], F[i], part[i][0], ALU.subtract).then_inc(f_res, 1)
                dve.wait_ge(f_mid, n + 1)
                dve.tensor_tensor(part[i][2], R[i], part[i][1], ALU.subtract).then_inc(f_lo, 1)

            dve.sem_inc(oo_saved, 1)
            with dve.Fori(0, G // 2) as k:
                def move(u):
                    dve.wait_ge(pT_ready, 16 * k + u + 1)
                    dve.tensor_copy(PTS[u % 2][:, HALF:N], bank(5)).then_inc(pTd_saved, 1)

                def norm(u):
                    dve.wait_ge(oo_ready, 16 * k + u + 1)
                    dve.reciprocal(arec[u % 2][:, :], asum[u % 4][:, :]).then_inc(rec_done, 1)
                    dve.wait_ge(rec_done, 16 * k + u + 1)
                    dve.tensor_scalar(RES[:, u % NK, 2 * k + u // NK, :], bank(6 + u % 2)[:, 0:D], arec[u % 2][:, :], None,
                                      ALU.mult).then_inc(oo_saved, 1)

                for u in range(16):
                    dve.wait_ge(sc_ready, 16 * k + u + 1)
                    dve.tensor_reduce(amax[u % 2][:, :], bank(2 * (u % 2), 2), AX.X, ALU.max).then_inc(max_done, 1)
                    dve.wait_ge(max_done, 16 * k + u + 1)
                    dve.tensor_scalar(aneg[u % 2][:, :], amax[u % 2][:, :], -SCALE, None, ALU.mult).then_inc(mx_ready, 1)
                    if u >= 1:
                        move(u - 1)
                    if u >= 2:
                        norm(u - 2)
                move(15)
                for u in (14, 15):
                    norm(u)
            for n in range(2 * T):
                b, ct, hf = n // 4, n // 2 % 2, n % 2
                xs = X[:, CT * b + ct, HALF * hf:HALF * (hf + 1)]
                dve.wait_ge(fin_ready, n + 1)
                dve.scalar_tensor_tensor(xs, bank(4 + n % 4), v("b_out", ct), xs, ALU.add, ALU.add).then_inc(fin_saved, 1)

        @block.tensor
        def _(pe):
            pe.wait_ge(bound_in, 1)
            pe.matmul(bank(0)[:, 0:1], w2l[:, :].bitcast(fp32), cs[:, 4:5], start=True, stop=True).then_inc(bound_ready, 1)
            pe.wait_ge(w2s_ready, 1)
            pe.wait_ge(ld_vec, 64)
            pe.transpose(bank(0)[:, 0:P], w2T[:, :], ident[:, :]).then_inc(w2sT_ready, 1)
            pe.wait_ge(w2_ready, 1)
            for t in range(T):
                pe.wait_ge(xn_ready, t + 1)
                for hf in range(2):
                    pe.matmul(bank(2 * t + hf), qw[:, t % CT, :], XN[:, t, HALF * hf:HALF * (hf + 1)],
                              start=True, stop=True).then_inc(q_ready, 1)
            pe.wait_ge(ld_vec, 64)
            for r in range(2 * T):
                pe.wait_ge(q_saved, r + 1)
                for i in range(4):
                    k = 4 * (r % 2) + i
                    last = pe.transpose(bank(r)[:, P * i:P * (i + 1)], XN[:, r // 2, P * k:P * (k + 1)], ident[:, :])
                last.then_inc(xT_ready, 1)
            pe.wait_ge(gelu_ready, 1)
            pe.wait_ge(pwl_ready, 1)
            pe.wait_ge(xT_saved, 2 * T)
            for t in range(T):
                last = pe.matmul(ps[0:2 * G, 0:J], pwl[:, t, :, :].rearrange("p c g -> p (c g)"), gel[:, 9 * t:9 * t + KD, :],
                                 start=(t == 0), stop=(t == T - 1))
            last.then_inc(pw_ready, 1)
            for k in range(NK):
                pe.wait_ge(ws_ready, k + 1)
                for t in range(T):
                    for h in range(HP):
                        g = HP * t + h
                        last = pe.matmul(ps[D * h:D * (h + 1), 512 + J * t:512 + J * (t + 1)],
                                         xnT[:, t, P * k + D * h:P * k + D * (h + 1)], wsm[:, k, J * g:J * (g + 1)],
                                         start=(k == 0 and t == 0), stop=(k == NK - 1), skip_group_check=True)
            last.then_inc(kv_ready, 1)
            pe.wait_ge(kv_saved, 1)
            for t in range(T):
                last = pe.matmul(bank(2)[:, J * t:J * (t + 1)], kw[:, t % CT, :], kvs[:, t, :], start=True, stop=True)
            last.then_inc(k_ready, 1)
            for t in range(T):
                last = pe.matmul(ps[0:J, 512 * 3 + P * t:512 * 3 + P * (t + 1)], kvs[:, t, :], vw[:, t % CT, :], start=True, stop=True)
            last.then_inc(v_ready, 1)
            pe.wait_ge(k_saved, 1)
            pe.wait_ge(q_copied, T)
            for g in range(G):
                t, h = g // HP, g % HP
                if g >= 4:
                    pe.wait_ge(qk_saved, g - 3)
                for i in range(NK):
                    last = pe.matmul(bank(4 + g % 4)[:, J * i:J * (i + 1)], XN[D * h:D * (h + 1), t, P * i:P * (i + 1)],
                                     ks[D * h:D * (h + 1), t, :], start=True, stop=True)
                last.then_inc(qk_ready, 1)

            def layer1(m, g):
                c, q, hf = m // 8, m % 8 // 2, m % 2
                if m % 8 == 0:
                    pe.wait_ge(mv_ready, CHUNKS * g + c + 1)
                pe.matmul(bank(m % 2), wl1[32 * q:32 * q + ROWS, :], mv[c % 2][32 * q:32 * q + ROWS, HALF * hf:HALF * (hf + 1)],
                          start=True, stop=True).then_inc(z1_ready, 1)

            def layer2(m, g):
                pe.wait_ge(h1l_ready, STEPS * g + m + 1)
                pe.matmul(bank(2 + m % 2), w2h[:, :], h1h[:, m % RING, :], start=True, stop=False)
                pe.matmul(bank(2 + m % 2), w2h[:, :], h1l[:, m % RING, :], start=False, stop=False)
                pe.matmul(bank(2 + m % 2), w2l[:, :], h1h[:, m % RING, :], start=False, stop=True).then_inc(z2_ready, 1)

            def layer3(m, g):
                c, q, hf = m // 8, m % 8 // 2, m % 2
                if m % RING == RING - 1:
                    pe.wait_ge(h2l_dve, STEPS // RING * g + (m + 1) // RING)
                else:
                    pe.wait_ge(h2l_pool, (STEPS - STEPS // RING) * g + m + 1 - (m + 1) // RING)
                for i in range(4):
                    a = J * (4 * hf + i) + 8 * q + c
                    pe.matmul(bank(4)[:, a:a + 33:32], h2h[m % RING][:, P * i:P * (i + 1)], w3s[:, :], start=True, stop=False)
                    last = pe.matmul(bank(4)[:, a:a + 33:32], h2l[m % RING][:, P * i:P * (i + 1)], w3s[:, :], start=False, stop=True)
                return last

            pe.wait_ge(w1_in, 16 * (4 * NR + 6))
            pe.wait_ge(qk_saved, G)
            layer1(0, 0)
            layer1(1, 0)
            for m in range(AHEAD2):
                if m >= 2:
                    pe.wait_ge(h2_ready, m - 1)
                layer2(m, 0)
                layer1(m + 2, 0)
            with pe.Fori(0, G) as g:
                for i in range(STEPS):
                    pe.wait_ge(h2_ready, STEPS * g + i + AHEAD2 - 1)
                    layer2(i + AHEAD2, g)
                    layer1(i + AHEAD1, g)
                    if i == 0:
                        pe.wait_ge(bias_saved, g + 1)
                    last = layer3(i, g)
                last.then_inc(bias_ready, 1)

            for g in range(G):
                t, h = g // HP, g % HP
                pe.wait_ge(normed, t + 1)
                if g == 0:
                    pe.wait_ge(h1l_ready, STEPS * G + AHEAD1)
                    pe.wait_ge(h2_ready, STEPS * G + AHEAD2)
                    pe.wait_ge(h2l_pool, (STEPS - STEPS // RING) * G + AHEAD2)
                if g >= 2:
                    pe.wait_ge(aT_saved, g - 1)
                for i in range(NK):
                    last = pe.transpose(ps[0:J, 1024 * (g % 2) + P * i:1024 * (g % 2) + P * (i + 1)],
                                        SIM[:, g, J * i:J * (i + 1)], ident[:, :])
                last.then_inc(aT_ready, 1)
                pe.wait_ge(aT_saved, g + 1)
                if h == 0 and t >= 2:
                    pe.wait_ge(o_saved, t - 1)
                for hf in range(2):
                    a = 512 * (4 + 2 * (t % 2) + hf)
                    last = pe.matmul(ps[D * h:D * (h + 1), a:a + HALF], vs[:, t, D * h:D * (h + 1)],
                                     att[g % 2][:, HALF * hf:HALF * (hf + 1)], start=True, stop=True)
                if h == HP - 1:
                    last.then_inc(o_ready, 1)
            pe.wait_ge(ld_late, 16 * 6)
            pe.wait_ge(o_saved, T)
            for n in range(T):
                b, hf = n // 2, n % 2
                for ct in range(CT):
                    r = CT * n + ct
                    if r >= 4:
                        pe.wait_ge(x1_ready, r - 3)
                    for kt in range(CT):
                        last = pe.matmul(bank(r % 4), outw[:, kt, P * ct:P * (ct + 1)], ao[:, CT * b + kt, HALF * hf:HALF * (hf + 1)],
                                         start=(kt == 0), stop=(kt == CT - 1))
                    last.then_inc(y_ready, 1)
            pe.wait_ge(x1_ready, 2 * T)
            for n in range(T):
                b, hf = n // 2, n % 2
                pe.wait_ge(xn2_ready, CT * (n + 1))
                for f in range(FT):
                    r = FT * n + f
                    if r >= 4:
                        pe.wait_ge(hid_saved, r - 3)
                    for kt in range(CT):
                        last = pe.matmul(bank(f % 4), m1[:, kt, P * f:P * (f + 1)], XN[:, CT * b + kt, HALF * hf:HALF * (hf + 1)],
                                         start=(kt == 0), stop=(kt == CT - 1))
                    last.then_inc(hid_ready, 1)
                pe.wait_ge(hid_saved, FT * (n + 1))
                for ct in range(CT):
                    r = CT * n + ct
                    if r >= 4:
                        pe.wait_ge(x2_ready, r - 3)
                    for f in range(FT):
                        last = pe.matmul(bank(4 + r % 4), m2[:, f, P * ct:P * (ct + 1)], hm[:, f, :],
                                         start=(f == 0), stop=(f == FT - 1))
                    last.then_inc(m_ready, 1)

            pe.wait_ge(x2_ready, 2 * T)
            wv = wqkv[:, :, :].rearrange("p t (k n) -> p t k n", k=3)
            for n in range(2 * NK):
                b, jt = n // NK, n % NK
                if n >= 4:
                    pe.wait_ge(vv_saved, n - 3)
                for kt in range(CT):
                    last = pe.matmul(bank(4 + n % 4)[:, 0:C], X[:, CT * b + kt, P * jt:P * (jt + 1)], wv[:, kt, 2, :],
                                     start=(kt == 0), stop=(kt == CT - 1))
                last.then_inc(vv_ready, 1)
            for n in range(2 * T):
                which, t = n // T, n % T
                b, mt = t // CT, t % CT
                if n >= 2:
                    pe.wait_ge(f_ready, n - 1)
                for hf in range(2):
                    for kt in range(CT):
                        last = pe.matmul(bank(2 * (n % 2) + hf), wv[:, kt, which, P * mt:P * (mt + 1)],
                                         X[:, CT * b + kt, HALF * hf:HALF * (hf + 1)], start=(kt == 0), stop=(kt == CT - 1))
                last.then_inc(p_ready, 1)

            def scores(u):
                i, it = u // NK, u % NK
                for jh in range(2):
                    for st in range(2):
                        last = pe.matmul(bank(2 * (u % 2) + jh), QS[i][st][:, P * it:P * (it + 1)],
                                         KS[i][st][:, HALF * jh:HALF * (jh + 1)], start=(st == 0), stop=(st == 1))
                last.then_inc(sc_ready, 1)

            def weigh(u, k):
                pe.wait_ge(pTa_saved, 16 * k + u + 1)
                pe.wait_ge(pTd_saved, 16 * k + u + 1)
                pe.wait_ge(oo_saved, 16 * k + max(u - 1, 0) + 1)
                for jt in range(NK):
                    last = pe.matmul(bank(6 + u % 2)[:, 0:D], PTS[u % 2][:, P * jt:P * (jt + 1)], V[:, jt, 2 * k + u // NK, :],
                                     start=(jt == 0), stop=(jt == NK - 1))
                last.then_inc(oo_ready, 1)

            pe.wait_ge(vv_saved, 2 * NK)
            pe.wait_ge(f_ready, 2 * T)
            with pe.Fori(0, G // 2) as k:
                pe.wait_ge(st_in[0], 256 * k + 256)
                scores(0)
                for u in range(16):
                    if u + 1 == NK:
                        pe.wait_ge(st_in[1], 256 * k + 256)
                    if u + 1 < 16:
                        if u >= 1:
                            pe.wait_ge(pr_ready, 16 * k + u)
                        scores(u + 1)
                    if u >= 1:
                        weigh(u - 1, k)
                    pe.wait_ge(pr_ready, 16 * k + u + 1)
                    for jt in range(NK):
                        last = pe.transpose(bank(4, 2)[:, P * jt:P * (jt + 1)], PR[u % 2][:, P * jt:P * (jt + 1)], ident[:, :])
                    last.then_inc(pT_ready, 1)
                weigh(15, k)
            pe.wait_ge(oo_saved, 16 * (G // 2) + 1)
            for n in range(2 * T):
                t, hf = n // 2, n % 2
                b, ct = t // CT, t % CT
                if n >= 4:
                    pe.wait_ge(rT_saved, n - 3)
                for i in range(4):
                    last = pe.transpose(bank(n % 4)[:, P * i:P * (i + 1)],
                                        RES[:, 4 * hf + i, NH * b + HP * ct:NH * b + HP * (ct + 1), :].rearrange("p n d -> p (n d)"),
                                        ident[:, :])
                last.then_inc(rT_ready, 1)
            for n in range(2 * T):
                b, ct, hf = n // 4, n // 2 % 2, n % 2
                pe.wait_ge(rT_saved, 4 * b + 4)
                if n >= 4:
                    pe.wait_ge(fin_saved, n - 3)
                for kt in range(CT):
                    last = pe.matmul(bank(4 + n % 4), wout[:, kt, P * ct:P * (ct + 1)], rT[:, CT * b + kt, HALF * hf:HALF * (hf + 1)],
                                     start=(kt == 0), stop=(kt == CT - 1))
                last.then_inc(fin_ready, 1)


def kernel(**inputs):
    import numpy as _np
    import concourse.bacc as _bacc
    from concourse import mybir as _mybir
    from concourse.bass_utils import run_bass_kernel_spmd as _run

    a = {k: _np.asarray(v) for k, v in inputs.items()}
    L0, L1 = "L0_conv_", "L1_conv_"

    def col(x):
        return x.reshape(-1, P).T

    def rep(x, n):
        return _np.tile(x, (n, 1))

    bqkv = a[L1 + "b_qkv"].reshape(NH, 3, D)
    part = _np.arange(P)
    vecs = _np.concatenate([
        col(a[L0 + "bn1_g"]), col(a[L0 + "bn1_b"]), col(a[L0 + "bn2_g"]), col(a[L0 + "bn2_b"]), col(a[L0 + "out_b"]),
        col(a[L0 + "mlp_b2"]), col(a[L1 + "b_out"]), col(a[L0 + "mlp_b1"]),
        rep(a[L0 + "off_dw_w"].reshape(D, TAPS * TAPS), HP), rep(a[L0 + "off_dw_b"].reshape(D, 1), HP),
        rep(a[L0 + "cpb_b1"].reshape(CH, 1), 2), rep(a[L0 + "cpb_b2"].reshape(CH, 1), 2),
        rep(a[L0 + "cpb_w1"].T, 2), rep(a[L0 + "cpb_w3"], 2), (part % 32 // 3 == 8).astype(_np.float32).reshape(P, 1),
        rep(a[L0 + "cpb_b3"].reshape(1, 1), P),
        rep(a[L0 + "off_pw_w"].T, HP), col(bqkv[:, 0].reshape(-1)), col(bqkv[:, 1].reshape(-1)),
        (part % W).reshape(P, 1).astype(_np.float32),
        (4 * _np.arange(NK)[None, :] + (part // W)[:, None]).astype(_np.float32)], axis=1)
    j = _np.arange(J)
    gq = (2.0 * _np.arange(W, dtype=_np.float32) / _np.float32(W - 1) - 1.0).astype(_np.float32)
    arrays = {
        "x": a["x"].reshape(B, C, N), "vecs": vecs, "ident": _np.eye(P, dtype=_np.float32),
        "gridj": _np.concatenate([_np.tile(j % KD, (G, 1)), _np.tile(j // KD, (G, 1))]).astype(_np.float32),
        "gridq": _np.tile(gq, (2 * G, 1)),
        "qwT": a[L0 + "qw"].transpose(0, 2, 1), "kwT": a[L0 + "kw"].transpose(0, 2, 1), "vwT": a[L0 + "vw"].transpose(0, 2, 1),
        "cw1": _np.concatenate([a[L0 + "cpb_w1"], a[L0 + "cpb_b1"].reshape(1, CH)]), "cw2": a[L0 + "cpb_w2"], "cw2T": a[L0 + "cpb_w2"].T,
        "out_wT": a[L0 + "out_w"].T, "m1T": a[L0 + "mlp_w1"].T, "m2T": a[L0 + "mlp_w2"].T,
        "wqkv": a[L1 + "W_qkv"].reshape(C, NH, 3, D).transpose(0, 2, 1, 3).reshape(C, 3 * C), "wout": a[L1 + "W_out"], "bv": bqkv[:, 2],
    }
    arrays = {k: _np.ascontiguousarray(v) for k, v in arrays.items()}
    nc = _bacc.Bacc("TRN2", target_bir_lowering=False, num_devices=1)
    d = {k: nc.dram_tensor("in_" + k, v.shape, _mybir.dt.from_np(v.dtype), kind="ExternalInput").ap() for k, v in arrays.items()}
    out = nc.dram_tensor("out", (B, C, N), _mybir.dt.float32, kind="ExternalOutput").ap()
    build(nc, d, out)
    r = _run(nc, [{"in_" + k: v for k, v in arrays.items()}], core_ids=[0])
    return _np.asarray(r.results[0]["out"]).reshape(B, C, H, W)
```

```python
import concourse.bass as bass
from concourse import mybir
from contextlib import ExitStack
import numpy as np

P = 128
B, C, H, W = 2, 256, 32, 32
N = H * W
CT = C // P
T = B * CT
NH, D = 8, 32
G = B * NH
HP = P // D
KD = 8
J = KD * KD
FT = 4 * C // P
TAPS, STRIDE = 6, 4
PADW, PADR = W + 2, 36
CH = 64
HALF = N // 2
NK = N // P
BN_INV = 1.0 / float(np.sqrt(np.float32(1.0 + 1e-5)))
SCALE = D ** -0.5

CHUNKS, STEPS = 8, 64
PARTS_S = [0, 0, 1, 1, 0, 2]
PARTS_W = [0, 1, 0, 1, 2, 0]
NR = len(PARTS_S)
ROWS = 16 + 2 * NR
RING = 4
AHEAD2 = 3
AHEAD1 = AHEAD2 + RING
LOG_MAX = 1.5

Q_STACK, K_STACK = [0, 0, 1, 1], [0, 1, 0, 1]
VW = 3 * D + 1
PSCALE = 2.0 ** 12
WS_POOL = 4
UNITS = 2 * NK

VEC = {}
_at = 0
for _n, _w in [("bn1_g", 2), ("bn1_b", 2), ("bn2_g", 2), ("bn2_b", 2), ("out_b", 2), ("mlp_b2", 2), ("b_out", 2),
               ("mlp_b1", 8), ("dw_w", 36), ("dw_b", 1), ("cb1", 1), ("cb2", 1), ("cw1T", 2), ("cw3", 1), ("one_rows", 1), ("cb3", 1), ("pw", 2),
               ("bq", 2), ("bk", 2), ("px", 1), ("py", 8)]:
    VEC[_n] = (_at, _w)
    _at += _w
NVEC = _at


def build(nc, d, out):
    fp32, bf16, fp16, fp32r = mybir.dt.float32, mybir.dt.bfloat16, mybir.dt.float16, mybir.dt.float32r
    i32 = mybir.dt.int32
    ALU, ACT, AX = mybir.AluOpType, mybir.ActivationFunctionType, mybir.AxisListType

    ctx = ExitStack()
    with ctx:
        def sb(name, shape, dt=fp32):
            return ctx.enter_context(nc.sbuf_tensor(name, shape, dt))

        def sem(name):
            return ctx.enter_context(nc.semaphore(name))

        def dram(name, shape, dt):
            return nc.dram_tensor(name, shape, dt, kind="Internal").ap()

        grid_d = dram("grid_d", [2 * G, J], fp32)
        s_d = dram("s_d", [3, 2, G, J * W], bf16)
        w1_d = dram("w1_d", [3, 3, CH], bf16)
        q_d = dram("q_d", [2, G * D, N], fp32)
        k_d = dram("k_d", [2, G * D, N], fp32)

        vec = sb("vec", [P, NVEC])
        ident = sb("ident", [P, P])
        gridj = sb("gridj", [2 * G, J])
        gridq = sb("gridq", [2 * G, W])
        X = sb("X", [P, T, N])
        XN = sb("XN", [P, T, N])
        qpad = sb("qpad", [P, T * PADR + 4, PADW])
        qw = sb("qw", [P, CT, P])
        kw = sb("kw", [P, CT, P])
        vw = sb("vw", [P, CT, P])
        outw = sb("outw", [P, CT, C])
        m1 = sb("m1", [P, CT, 4 * C])
        m2 = sb("m2", [P, FT, C])
        late = qpad[:, :, :].rearrange("p a b -> p (a b)")
        wqkv = late[:, 0:CT * 3 * C].rearrange("p (t n) -> p t n", t=CT)
        wout = late[:, CT * 3 * C:CT * 4 * C].rearrange("p (t n) -> p t n", t=CT)
        bv = sb("bv", [P, NH, D])
        sc = sb("sc", [P, 4])
        conv = sb("conv", [P, T * 9, KD])
        gel = sb("gel", [P, T * 9, KD])
        pwl = sb("pwl", [P, T, 2, G])
        off = sb("off", [2 * G, J])
        vpos = sb("vpos", [2 * G, J])
        npos = sb("npos", [2 * G, J])
        gxy = sb("gxy", [2 * G, J])
        w1s = sb("w1s", [3, CH])
        w1r = sb("w1r", [3, CH])
        w1p = sb("w1p", [3, 3, CH], bf16)
        wl1 = sb("wl1", [P, P], bf16)
        w2bd = sb("w2bd", [P, P])
        w2T = sb("w2T", [P, P])
        w2h, w2l = sb("w2h", [P, P], fp32r), sb("w2l", [P, P], fp32r)
        w3s = sb("w3s", [P, 2 * P], bf16)
        cs = sb("cs", [P, 12])
        sx = sb("sx", [P, G + 1, CHUNKS, W], bf16)
        sy = sb("sy", [P, G + 1, CHUNKS, W], bf16)
        BT = sb("BT", [P, G, HALF])
        big = sb("big", [P, 12, N])
        kvs = sb("kvs", [P, T, J])
        ks = sb("ks", [P, T, HP, J])
        vs = sb("vs", [P, T, 2, 2 * D])
        mv = [sb(f"mv{i}", [P, N], bf16) for i in range(2)]
        gb = m1[:, :, :]
        hx = m2[:, 0:4, :].rearrange("p a b -> p (a b)")
        h1h, h1l = sb("h1h", [P, RING, HALF], fp32r), sb("h1l", [P, RING, HALF], fp32r)
        h2 = [big[:, i // 2, HALF * (i % 2):HALF * (i % 2 + 1)] for i in range(RING)]
        h2h = [big[:, 2, 256 * i:256 * (i + 1)].bitcast(fp16) for i in range(RING)]
        h2l = [big[:, 3, 256 * i:256 * (i + 1)].bitcast(fp16) for i in range(RING)]
        smax, ssum, srec = ([sb(f"{n}{i}", [P, NK]) for i in range(2)] for n in ("smax", "ssum", "srec"))

        pos = BT[0:2 * G, 0:4, :].rearrange("p a b -> p (a b)")
        pp = BT[0:2 * G, 4:8, :].rearrange("p a b -> p (a b)")
        pn = BT[0:2 * G, 8:12, :].rearrange("p a b -> p (a b)")
        s3 = BT[0:2 * G, 12:16, :].rearrange("p a b -> p (a b)")
        xnT = big[:, 0:4, :]
        wsm = big[:, 4:12, :]
        att = [big[:, r:r + 2, :].rearrange("p h (c q) -> p h c q", c=2) for r in (0, 6)]
        prob = [big[:, 10 + i // 2, HALF * (i % 2):HALF * (i % 2 + 1)] for i in range(4)]
        ao = big[:, 2:6, :]
        hm = big[:, 6:10, :].rearrange("p a b -> p (a b)").rearrange("p (f n) -> p f n", f=FT)
        spt = [qpad[:, :, :].rearrange("p a b -> p (a b)")[0:2 * G, N * a:N * (a + 1)].bitcast(bf16) for a in range(3)]

        ps = ctx.enter_context(nc.psum_tensor("ps", [P, 8 * 512], fp32))

        def bank(i, n=1):
            return ps[:, 512 * i:512 * (i + n)]

        z1 = [bank(i) for i in (0, 1, 5, 6)]
        z2 = [bank(i) for i in (2, 3)]

        def v(name, i=0, n=1):
            a = VEC[name][0] + i
            return vec[:, a:a + n]

        ld_vec, ld_bd, ld_w1, ld_late = (sem(x) for x in ("ld_vec", "ld_bd", "ld_w1", "ld_late"))
        ld_x = [sem(f"ld_x{b}") for b in range(B)]
        cleared = sem("cleared")
        dve_chain = sem("dve_chain")
        scales_ready, xn_ready, q_ready, q_saved = (sem(x) for x in ("scales_ready", "xn_ready", "q_ready", "q_saved"))
        xT_ready, xT_saved, conv_ready, gelu_ready = (sem(x) for x in ("xT_ready", "xT_saved", "conv_ready", "gelu_ready"))
        pwl_ready, pw_ready, off_ready, gxy_ready = (sem(x) for x in ("pwl_ready", "pw_ready", "off_ready", "gxy_ready"))
        grid_out, grid_in, w1p_ready, w1_out, w1_in = (sem(x) for x in ("grid_out", "grid_in", "w1p_ready", "w1_out", "w1_in"))
        pn_ready, ln_ready, sparts_ready, s_in = (sem(x) for x in ("pn_ready", "ln_ready", "sparts_ready", "s_in"))
        s_out = [sem(f"s_out{a}") for a in range(3)]
        ws_ready, kv_ready, kv_saved, k_ready, v_ready, k_saved, v_saved = (
            sem(x) for x in ("ws_ready", "kv_ready", "kv_saved", "k_ready", "v_ready", "k_saved", "v_saved"))
        abs_ready, hat_ready, ws_pool = sem("abs_ready"), sem("hat_ready"), sem("ws_pool")
        q_copied, qk_ready = sem("q_copied"), sem("qk_ready")
        mv_ready, z1_ready, h1h_ready, h1l_ready, z2_ready, h2_ready, h2h_ready = (
            sem(x) for x in ("mv_ready", "z1_ready", "h1h_ready", "h1l_ready", "z2_ready", "h2_ready", "h2h_ready"))
        h2l_pool, h2l_dve, bias_ready, bias_saved = (sem(x) for x in ("h2l_pool", "h2l_dve", "bias_ready", "bias_saved"))
        bound_in, bound_ready, w2s_ready, w2sT_ready, w2_ready = (
            sem(x) for x in ("bound_in", "bound_ready", "w2s_ready", "w2sT_ready", "w2_ready"))
        max_found, max_moved, sum_found, sum_inverted = (sem(x) for x in ("max_found", "max_moved", "sum_found", "sum_inverted"))
        shifted, exped, normed, aT_ready, aT_saved, o_ready, o_saved = (
            sem(x) for x in ("shifted", "exped", "normed", "aT_ready", "aT_saved", "o_ready", "o_saved"))
        y_ready, x1_ready, xn2_ready, hid_ready, hid_saved, m_ready, x2_ready = (
            sem(x) for x in ("y_ready", "x1_ready", "xn2_ready", "hid_ready", "hid_saved", "m_ready", "x2_ready"))
        p_ready, f_hi, f_lo = (sem(x) for x in ("p_ready", "f_hi", "f_lo"))
        parts_out = [sem("parts_out0"), sem("parts_out1")]
        rec_done, qw_scaled, kv_cleared = sem("rec_done"), sem("qw_scaled"), sem("kv_cleared")
        vv_ready, vv_saved = sem("vv_ready"), sem("vv_saved")
        st_in = [sem("st_in0"), sem("st_in1")]
        sc_ready, mx_ready, pr_ready, pT_ready, pTh_ready, pTl_ready, oo_ready, oo_saved = (
            sem(x) for x in ("sc_ready", "mx_ready", "pr_ready", "pT_ready", "pTh_ready", "pTl_ready", "oo_ready", "oo_saved"))
        pF_ready, pFh_ready, pFl_ready = sem("pF_ready"), sem("pFh_ready"), sem("pFl_ready")
        v_done = sem("v_done")
        sums_column, o_sum, o_done = sem("sums_column"), sem("o_sum"), sem("o_done")
        rT_ready, rT_saved, fin_ready, fin_saved, stored = (
            sem(x) for x in ("rT_ready", "rT_saved", "fin_ready", "fin_saved", "stored"))

        V = big[:, 0:4, :].rearrange("p a b -> p (a b)").rearrange("p (n j d) -> p n j d", j=NK, n=G)
        V3 = BT[:, 0:13, :].rearrange("p a b -> p (a b)").bitcast(bf16)[:, 0:NK * G * VW].rearrange("p (n j w) -> p n j w", j=NK, n=G)
        VR = big[:, 4:8, :].rearrange("p a b -> p (a b)").rearrange("p (n j d) -> p n j d", j=NK, n=G)
        RES = big[:, 4:8, :].rearrange("p a b -> p (a b)").rearrange("p (i n d) -> p i n d", i=NK, n=G)
        rT = XN
        PR = [big[:, 8, :], big[:, 9, :]]
        PTH = [big[:, 10, HALF * i:HALF * (i + 1)].bitcast(fp16) for i in range(2)]
        PTL = [big[:, 11, HALF * i:HALF * (i + 1)].bitcast(fp16) for i in range(2)]
        PF = [BT[:, 14 + i, :] for i in range(2)]
        part = [[XN[:, 2 * i + a, :].bitcast(fp32r) for a in range(2)] for i in range(2)]
        QS = [h1h[:, 2 * i:2 * i + 2, :].rearrange("p a b -> p (a b)") for i in range(2)]
        KS = [h1l[:, 2 * i:2 * i + 2, :].rearrange("p a b -> p (a b)") for i in range(2)]
        O3 = [BT[:, 13, P * i:P * i + 3 * D] for i in range(2)]
        OS = [BT[:, 13, 256 + D * i:256 + D * (i + 1)] for i in range(2)]
        aneg = [sb(f"aneg{i}", [P, 1]) for i in range(2)]
        arec = [sb(f"arec{i}", [P, 1]) for i in range(2)]

        out_v = out.rearrange("b (c p) n -> p b c n", p=P)
        x_v = d["x"].rearrange("b (c p) n -> p b c n", p=P)

        block = ctx.enter_context(nc.Block())

        @block.sync
        def _(sp):
            sp.dma_start(vec[:, :], d["vecs"]).then_inc(ld_vec, 16)
            for b in range(B):
                sp.dma_start(X[:, CT * b:CT * (b + 1), :], x_v[:, b]).then_inc(ld_x[b], 16)
            sp.dma_start(ident[:, :], d["ident"]).then_inc(ld_vec, 16)
            sp.dma_start(gridj[:, :], d["gridj"]).then_inc(ld_vec, 16)
            sp.dma_start(gridq[:, :], d["gridq"]).then_inc(ld_vec, 16)
            sp.wait_ge(cleared, 6)
            for w, src in ((qw, "qwT"), (kw, "kwT"), (vw, "vwT")):
                for h in range(HP):
                    sp.dma_start(w[D * h:D * (h + 1), :, D * h:D * (h + 1)],
                                 d[src].rearrange("(t h) c o -> h c t o", h=HP)[h]).then_inc(ld_bd, 16)
            for h in range(2):
                sp.dma_start(w2bd[CH * h:CH * (h + 1), CH * h:CH * (h + 1)], d["cw2"]).then_inc(ld_bd, 16)
                sp.dma_start(w2T[CH * h:CH * (h + 1), CH * h:CH * (h + 1)], d["cw2T"]).then_inc(ld_bd, 16)
            sp.wait_ge(w1p_ready, 1)
            sp.dma_start(w1_d, w1p[:, :, :]).then_inc(w1_out, 16)
            sp.wait_ge(w1_out, 16)
            for jh in range(2):
                for c in range(2):
                    for r in range(NR):
                        row = 16 * jh + NR * c + r
                        sp.dma_start(wl1[row:row + 97:32, CH * jh:CH * (jh + 1)],
                                     w1_d[c, PARTS_W[r]:PARTS_W[r] + 1, :].to_broadcast((4, CH))).then_inc(w1_in, 16)
                for a in range(3):
                    sp.dma_start(wl1[2 * NR + a:2 * NR + a + 97:32, CH * jh:CH * (jh + 1)],
                                 w1_d[2, a:a + 1, :].to_broadcast((4, CH))).then_inc(w1_in, 16)
            sp.wait_ge(gxy_ready, 1)
            sp.dma_start(grid_d, gxy[:, :]).then_inc(grid_out, 16)
            sp.wait_ge(grid_out, 16)
            sp.dma_start(gb[:, :, :].rearrange("p a b -> p (a b)"),
                         grid_d.rearrange("a b -> (a b)").partition_broadcast(P)).then_inc(grid_in, 16)
            sv = s_d.rearrange("a c g (m n) -> a c m g n", m=8)

            def send(a):
                sp.wait_ge(sparts_ready, a + 1)
                sp.dma_start(s_d[a].rearrange("c g n -> (c g) n"), spt[a]).then_inc(s_out[a], 16)

            def place(c, r):
                dst = (sx, sy)[c]
                row = NR * c + r
                sp.dma_start(dst[row:row + 113:16, 0:G, :, :].rearrange("p g a b -> p g (a b)"), sv[PARTS_S[r], c]).then_inc(s_in, 16)

            send(0)
            sp.wait_ge(s_out[0], 16)
            sp.wait_ge(cleared, 9 + G + 1)
            rows = [[(c, r) for r in range(NR) if PARTS_S[r] == a for c in range(2)] for a in range(3)]
            for c, r in rows[0][:3]:
                place(c, r)
            send(1)
            for c, r in rows[0][3:]:
                place(c, r)
            sp.wait_ge(s_out[1], 16)
            send(2)
            for c, r in rows[1]:
                place(c, r)
            sp.wait_ge(s_out[2], 16)
            for c, r in rows[2]:
                place(c, r)
            sp.wait_ge(ws_pool, WS_POOL)
            sp.wait_ge(ws_ready, NK - WS_POOL)
            sp.wait_ge(q_copied, T)
            for dst, src, n in ((outw, "out_wT", CT), (m1, "m1T", CT), (m2, "m2T", FT), (wqkv, "wqkv", CT), (wout, "wout", CT)):
                sp.dma_start(dst[:, :, :], d[src].rearrange("(t p) n -> p t n", p=P)).then_inc(ld_late, 16)
            sp.dma_start(bv[:, :, :], d["bv"].partition_broadcast(P)).then_inc(ld_late, 16)

            def send_parts(n):
                which, t = n % 2, n // 2
                dst = (q_d, k_d)[which]
                for a, ready in enumerate((f_hi, f_lo)):
                    sp.wait_ge(ready, n + 1)
                    sp.dma_start(dst[a, P * t:P * (t + 1), :], part[which][a].bitcast(fp32)).then_inc(parts_out[which], 16)

            def load_head(i, n):
                for r in range(HP):
                    sp.dma_start(QS[i][D * r:D * (r + 1), :].bitcast(fp32), q_d[Q_STACK[r], bass.ds(n * D, D), :]).then_inc(st_in[i], 16)
                    sp.dma_start(KS[i][D * r:D * (r + 1), :].bitcast(fp32), k_d[K_STACK[r], bass.ds(n * D, D), :]).then_inc(st_in[i], 16)

            for n in range(6):
                send_parts(n)
            for i in range(2):
                sp.wait_ge(parts_out[i], 32 * 3)
            load_head(0, 0)
            load_head(1, 1)
            for n in range(6, 2 * T):
                send_parts(n)
            for i in range(2):
                sp.wait_ge(parts_out[i], 32 * T)
            with sp.Fori(0, G // 2 - 1) as k:
                sp.wait_ge(sc_ready, UNITS * k + NK)
                load_head(0, 2 * k + 2)
                sp.wait_ge(sc_ready, UNITS * k + 2 * NK)
                load_head(1, 2 * k + 3)
            sp.wait_ge(sc_ready, UNITS * (G // 2 - 1) + NK)
            sp.sem_inc(st_in[0], 16 * 2 * HP)

            for n in range(T):
                for hf in range(2):
                    sp.wait_ge(fin_saved, 2 * n + hf + 1)
                    sp.dma_start(out_v[:, n // CT, n % CT, HALF * hf:HALF * (hf + 1)],
                                 X[:, n, HALF * hf:HALF * (hf + 1)]).then_inc(stored, 16)
            sp.wait_ge(stored, 16 * 2 * T)

        @block.gpsimd
        def _(pool):
            for m in (qw[:, :, :], kw[:, :, :], vw[:, :, :], w2T[:, :], w2bd[:, :], wl1[:, :],
                      qpad[:, :, :], pwl[:, :, :, :], sy[:, :, :, :]):
                pool.memset(m, 0.0).then_inc(cleared, 1)
            for m in (ks[:, :, :, :], vs[:, :, :, :]):
                pool.memset(m, 0.0).then_inc(kv_cleared, 1)
            pool.wait_ge(ld_vec, 64)
            for g in range(G + 1):
                pool.tensor_copy(sx[:, g, :, :], v("one_rows").unsqueeze(2).to_broadcast((P, CHUNKS, W))).then_inc(cleared, 1)

            def spread(i, g, jj):
                shape = (P, H, W)
                pool.tensor_tensor(mv[i][:, :].rearrange("p (a b) -> p a b", a=H),
                                   sx[:, g, jj, :].unsqueeze(1).to_broadcast(shape),
                                   sy[:, g, jj, :].unsqueeze(2).to_broadcast(shape), ALU.add).then_inc(mv_ready, 1)

            pool.wait_ge(q_saved, 2 * T)
            pool.wait_ge(xT_ready, 2 * T)
            for t in range(T):
                row = PADR * t + 1
                pool.tensor_copy(XN[:, t, :].rearrange("p (a b) -> p a b", b=W), qpad[:, row:row + H, 1:1 + W]).then_inc(q_copied, 1)

            for k in range(WS_POOL):
                pool.wait_ge(hat_ready, k + 2)
                pool.tensor_tensor(wsm[:, k, :], wsm[:, k, :], hx[:, :], ALU.mult).then_inc(ws_pool, 1)

            pool.wait_ge(s_in, 16 * 2 * NR)
            def low2(m):
                if m % RING != RING - 1:
                    pool.tensor_tensor(h2l[m % RING], h2[m % RING], h2h[m % RING], ALU.subtract).then_inc(h2l_pool, 1)

            spread(0, 0, 0)
            spread(1, 0, 1)
            for m in range(AHEAD2):
                pool.wait_ge(h2h_ready, m + 1)
                low2(m)
            with pool.Fori(0, G) as g:
                for m in range(AHEAD2, STEPS + AHEAD2):
                    if m % RING != RING - 1:
                        pool.wait_ge(h2h_ready, STEPS * g + m + 1)
                        low2(m)
                    if m % 8 == 6:
                        c = m // 8 + 2
                        pool.wait_ge(z1_ready, STEPS * g + 8 * (c - 1))
                        spread(c % 2, g + c // CHUNKS, c % CHUNKS)

            for u in range(G):
                pr = prob[u % 4].rearrange("p (i j) -> p i j", j=J)
                pool.wait_ge(sum_inverted, u + 1)
                pool.tensor_tensor(pr, pr, srec[u % 2][:, :].unsqueeze(2).to_broadcast((P, NK, J)), ALU.mult).then_inc(normed, 1)

            pool.wait_ge(ld_late, 16 * 6)
            pool.tensor_scalar(wqkv[:, :, 0:C], wqkv[:, :, 0:C], SCALE, None, ALU.mult).then_inc(qw_scaled, 1)
            pool.tensor_scalar(v("bq", 0, CT), v("bq", 0, CT), SCALE, None, ALU.mult).then_inc(qw_scaled, 1)

            pool.wait_ge(aT_ready, G)
            pool.memset(V3[:, :, :, 3 * D:VW], 1.0 / PSCALE).then_inc(sums_column, 1)

            def low0T(u):
                pool.tensor_tensor(PTL[u % 2][:, 0:HALF], PF[u % 2], PTH[u % 2][:, 0:HALF], ALU.subtract).then_inc(pFl_ready, 1)

            def add_up(u, k):
                pool.wait_ge(oo_saved, UNITS * k + u + 3)
                pool.tensor_tensor(OS[u % 2], O3[u % 2][:, 0:D], O3[u % 2][:, D:2 * D], ALU.add).then_inc(o_sum, 1)
                pool.wait_ge(o_sum, UNITS * k + u + 1)
                pool.tensor_tensor(RES[:, u % NK, 2 * k + u // NK, :], OS[u % 2], O3[u % 2][:, 2 * D:3 * D], ALU.add).then_inc(o_done, 1)

            pool.wait_ge(v_done, 4 * B)
            pool.sem_inc(o_done, 2)
            pool.wait_ge(pFh_ready, 1)
            pool.sem_inc(pFl_ready, 1)
            low0T(0)
            with pool.Fori(0, G // 2) as k:
                for i in range(UNITS):
                    pool.wait_ge(pFh_ready, UNITS * k + i + 2)
                    low0T(i + 1)
                    if i >= 1:
                        add_up(i - 1, k)
                add_up(UNITS - 1, k)

        @block.scalar
        def _(act):
            act.dma_start(w1s[:, :], d["cw1"]).then_inc(ld_w1, 16)
            act.wait_ge(scales_ready, 1)
            for t in range(T):
                act.wait_ge(ld_x[t // CT], 16)
                act.activation(XN[:, t, :], X[:, t, :], ACT.Identity, scale=sc[:, t % CT:t % CT + 1],
                               bias=v("bn1_b", t % CT)).then_inc(xn_ready, 1)
            for r in range(2 * T):
                act.wait_ge(xT_ready, r + 1)
                act.activation(xnT[:, r // 2, HALF * (r % 2):HALF * (r % 2 + 1)], bank(r), ACT.Identity).then_inc(xT_saved, 1)
            act.wait_ge(conv_ready, 1)
            act.activation(gel[:, :, :], conv[:, :, :], ACT.Gelu, bias=v("dw_b")).then_inc(gelu_ready, 1)
            act.wait_ge(pw_ready, 1)
            act.activation(off[:, :], ps[0:2 * G, 0:J], ACT.Tanh).then_inc(off_ready, 1)
            act.wait_ge(pn_ready, 1)
            act.activation(pp, pp, ACT.Ln, bias=1.0).then_inc(ln_ready, 1)
            act.wait_ge(pn_ready, 2)
            act.activation(pn, pn, ACT.Ln, bias=1.0).then_inc(ln_ready, 1)
            act.wait_ge(grid_in, 16)
            for i in range(NK + 1):
                dst, src, pixel = (hx[:, :], gb[:, 0, :], v("px")) if i == 0 else (wsm[:, i - 1, :], gb[:, 1, :], v("py", i - 1))
                act.activation(dst, src, ACT.Abs, scale=-1.0, bias=pixel).then_inc(abs_ready, 1)
                act.wait_ge(abs_ready, i + 1)
                act.activation(dst, dst, ACT.Relu, scale=-1.0, bias=1.0).then_inc(hat_ready, 1)
            act.wait_ge(kv_ready, 1)
            act.activation(kvs[:, :, :], bank(1)[:, 0:T * J].rearrange("p (t j) -> p t j", t=T), ACT.Identity).then_inc(kv_saved, 1)
            act.wait_ge(k_ready, 1)
            act.wait_ge(kv_cleared, 2)
            for h in range(HP):
                act.activation(ks[D * h:D * (h + 1), :, h, :], bank(2)[D * h:D * (h + 1), 0:T * J].rearrange("p (t j) -> p t j", t=T),
                               ACT.Identity, scale=SCALE).then_inc(k_saved, 1)
            act.wait_ge(v_ready, 1)
            for i in range(2):
                act.activation(vs[J * i:J * (i + 1), :, :, D * i:D * (i + 1)],
                               bank(3)[J * i:J * (i + 1), :].rearrange("p (t c o) -> p t c o", t=T, c=2)[:, :, :, D * i:D * (i + 1)],
                               ACT.Identity).then_inc(v_saved, 1)
            def high1(m):
                act.activation(h1h[:, m % RING, :], z1[m % RING], ACT.Relu).then_inc(h1h_ready, 1)

            def relu2(m):
                act.activation(h2[m % RING], z2[m % 2], ACT.Relu, bias=cs[:, 9:10]).then_inc(h2_ready, 1)

            for m in range(RING):
                act.wait_ge(z1_ready, m + 1)
                high1(m)
            act.wait_ge(w2_ready, 1)
            for m in range(AHEAD2):
                act.wait_ge(z2_ready, m + 1)
                relu2(m)
                act.wait_ge(z1_ready, m + RING + 1)
                high1(m + RING)
            with act.Fori(0, G) as g:
                for m in range(AHEAD2, STEPS + AHEAD2):
                    act.wait_ge(z2_ready, STEPS * g + m + 1)
                    relu2(m)
                    act.wait_ge(z1_ready, STEPS * g + m + RING + 1)
                    high1(m + RING)

            for u in range(G + 2):
                if u < G:
                    act.wait_ge(shifted, u + 1)
                    act.activation(prob[u % 4], prob[u % 4], ACT.Exp).then_inc(exped, 1)
                if u >= 2:
                    e = u - 2
                    t, i = e // 4, e % 4
                    act.wait_ge(aT_ready, e + 1)
                    if i == 0 and t >= 2:
                        act.wait_ge(o_ready, t - 1)
                    act.activation(att[t % 2][:, :, :, P * i:P * (i + 1)], bank(2 + e % 2).rearrange("p (h c q) -> p h c q", h=2, c=2),
                                   ACT.Identity).then_inc(aT_saved, 1)
                    if i == 1 and t >= 1:
                        act.wait_ge(o_ready, t)
                        act.activation(ao[:, t - 1, :], bank(4 + 2 * ((t - 1) % 2), 2), ACT.Identity).then_inc(o_saved, 1)
            act.wait_ge(o_ready, T)
            act.activation(ao[:, T - 1, :], bank(4 + 2 * ((T - 1) % 2), 2), ACT.Identity).then_inc(o_saved, 1)
            for n in range(T):
                for ct in range(CT):
                    b, hf = n // 2, n % 2
                    act.wait_ge(x1_ready, CT * n + ct + 1)
                    act.activation(XN[:, CT * b + ct, HALF * hf:HALF * (hf + 1)], X[:, CT * b + ct, HALF * hf:HALF * (hf + 1)],
                                   ACT.Identity, scale=sc[:, CT + ct:CT + ct + 1], bias=v("bn2_b", ct)).then_inc(xn2_ready, 1)
            for n in range(T):
                for f in range(FT):
                    act.wait_ge(hid_ready, FT * n + f + 1)
                    act.activation(hm[:, f, :], bank(f % 4), ACT.Gelu, bias=v("mlp_b1", f)).then_inc(hid_saved, 1)

            act.wait_ge(qw_scaled, 2)
            for n in range(2 * T):
                which, t = n % 2, n // 2
                i = n % 2
                act.wait_ge(p_ready, n + 1)
                if n >= 2:
                    act.wait_ge(f_lo, n - 1)
                    act.wait_ge(parts_out[i], 32 * (n // 2))
                act.activation(part[i][0], bank(2 * i, 2), ACT.Identity, bias=v(("bq", "bk")[which], t % CT)).then_inc(f_hi, 1)

            def exps(u):
                act.activation(PR[u % 2], bank(2 * (u % 2), 2), ACT.Exp, bias=aneg[u % 2][:, :]).then_inc(pr_ready, 1)

            def full0(u):
                act.activation(PF[u % 2], bank(4), ACT.Copy, scale=PSCALE).then_inc(pF_ready, 1)

            def high1T(u):
                act.activation(PTH[u % 2][:, HALF:N], bank(5), ACT.Copy, scale=PSCALE).then_inc(pTh_ready, 1)

            def outputs(u, k):
                act.wait_ge(oo_ready, UNITS * k + u + 1)
                act.wait_ge(rec_done, UNITS * k + u + 1)
                act.wait_ge(o_done, UNITS * k + u + 1)
                act.activation(O3[u % 2], bank(6 + u % 2)[:, 0:3 * D], ACT.Copy, scale=arec[u % 2][:, :]).then_inc(oo_saved, 1)

            act.sem_inc(oo_saved, 2)
            for u in range(2):
                act.wait_ge(mx_ready, u + 1)
                exps(u)
            act.wait_ge(pT_ready, 1)
            full0(0)
            act.wait_ge(pT_ready, 2)
            high1T(0)
            with act.Fori(0, G // 2) as k:
                for i in range(UNITS):
                    act.wait_ge(mx_ready, UNITS * k + i + 3)
                    exps(i + 2)
                    act.wait_ge(pT_ready, 2 * (UNITS * k + i + 1) + 1)
                    act.wait_ge(pFl_ready, UNITS * k + i + 1)
                    full0(i + 1)
                    act.wait_ge(pT_ready, 2 * (UNITS * k + i + 1) + 2)
                    high1T(i + 1)
                    if i >= 1:
                        outputs(i - 1, k)
                outputs(UNITS - 1, k)
            for n in range(2 * T):
                act.wait_ge(rT_ready, n + 1)
                act.activation(rT[:, n // 2, HALF * (n % 2):HALF * (n % 2 + 1)], bank(n % 4), ACT.Identity).then_inc(rT_saved, 1)

        @block.vector
        def _(dve):
            chain = [0]

            def link(ins):
                chain[0] += 1
                ins.then_inc(dve_chain, 1)
                dve.wait_ge(dve_chain, chain[0])

            dve.wait_ge(ld_vec, 64)
            dve.tensor_scalar(sc[:, 0:CT], v("bn1_g", 0, CT), BN_INV, None, ALU.mult).then_inc(scales_ready, 1)
            dve.tensor_scalar(sc[:, CT:2 * CT], v("bn2_g", 0, CT), BN_INV, None, ALU.mult)
            dve.wait_ge(ld_w1, 16)
            link(dve.tensor_copy(w1p[:, 0, :], w1s[:, :]))
            link(dve.tensor_tensor(w1r[:, :], w1s[:, :], w1p[:, 0, :], ALU.subtract))
            link(dve.tensor_copy(w1p[:, 1, :], w1r[:, :]))
            dve.tensor_tensor(w1p[:, 2, :], w1r[:, :], w1p[:, 1, :], ALU.subtract).then_inc(w1p_ready, 1)
            dve.wait_ge(cleared, 8)
            for h in range(HP):
                for t in range(T):
                    last = dve.tensor_copy(pwl[D * h:D * (h + 1), t, :, HP * t + h], vec[D * h:D * (h + 1), VEC["pw"][0]:VEC["pw"][0] + 2])
            last.then_inc(pwl_ready, 1)
            for r in range(2 * T):
                t, hf = r // 2, r % 2
                dve.wait_ge(q_ready, r + 1)
                row = PADR * t + 1 + (H // 2) * hf
                dve.tensor_copy(qpad[:, row:row + H // 2, 1:1 + W], bank(r).rearrange("p (a b) -> p a b", b=W)).then_inc(q_saved, 1)
            dve.wait_ge(q_saved, 2 * T)
            for tap in range(TAPS * TAPS):
                ky, kx = tap // TAPS, tap % TAPS
                src = qpad[:, ky:ky + STRIDE * (T * 9 - 1) + 1:STRIDE, kx:kx + STRIDE * (KD - 1) + 1:STRIDE]
                if tap == 0:
                    link(dve.tensor_scalar(conv[:, :, :], src, v("dw_w", 0), None, ALU.mult))
                else:
                    link(dve.scalar_tensor_tensor(conv[:, :, :], src, v("dw_w", tap), conv[:, :, :], ALU.mult, ALU.add))
            dve.sem_inc(conv_ready, 1)
            dve.wait_ge(off_ready, 1)
            link(dve.scalar_tensor_tensor(vpos[:, :], off[:, :], 4.0, gridj[:, :], ALU.mult, ALU.add))
            link(dve.tensor_scalar(npos[:, :], vpos[:, :], 2.0 / (KD - 1), -1.0, ALU.mult, ALU.add))
            link(dve.tensor_scalar(gxy[:, :], npos[:, :], 1.0, W / 2.0, ALU.add, ALU.mult))
            link(dve.tensor_scalar(gxy[:, :], gxy[:, :], -0.5, None, ALU.add))
            dve.sem_inc(gxy_ready, 1)
            shape = (2 * G, J, W)
            r3 = "p (j q) -> p j q"
            link(dve.tensor_tensor(pos.rearrange(r3, j=J), gridq[:, :].unsqueeze(1).to_broadcast(shape),
                                   npos[:, :].unsqueeze(2).to_broadcast(shape), ALU.subtract))
            dve.tensor_scalar(pp, pos, 0.0, None, ALU.max).then_inc(pn_ready, 1)
            dve.tensor_scalar(pn, pos, -1.0, 0.0, ALU.mult, ALU.max).then_inc(pn_ready, 1)
            dve.wait_ge(ld_bd, 16 * (3 * HP + 4))
            link(dve.tensor_scalar(w2h[:, :], w2bd[:, :], -1.0, None, ALU.mult))
            link(dve.tensor_tensor(w2l[:, :], w2bd[:, :], w2h[:, :].bitcast(fp32), ALU.max))
            link(dve.tensor_scalar(cs[:, 0:2], v("cw1T", 0, 2), -1.0, None, ALU.mult))
            link(dve.tensor_tensor(cs[:, 0:2], cs[:, 0:2], v("cw1T", 0, 2), ALU.max))
            link(dve.tensor_tensor(cs[:, 2:3], cs[:, 0:1], cs[:, 1:2], ALU.add))
            link(dve.tensor_scalar(cs[:, 3:4], v("cb1"), -1.0, None, ALU.mult))
            link(dve.tensor_tensor(cs[:, 3:4], cs[:, 3:4], v("cb1"), ALU.max))
            link(dve.scalar_tensor_tensor(cs[:, 4:5], cs[:, 2:3], LOG_MAX, cs[:, 3:4], ALU.mult, ALU.add))
            dve.sem_inc(bound_in, 1)
            dve.wait_ge(ln_ready, 2)
            link(dve.tensor_tensor(s3, pp, pn, ALU.subtract))
            dve.wait_ge(q_copied, T)
            dve.tensor_copy(spt[0], s3).then_inc(sparts_ready, 1)
            dve.wait_ge(sparts_ready, 1)
            link(dve.tensor_tensor(pos, s3, spt[0], ALU.subtract))
            dve.tensor_copy(spt[1], pos).then_inc(sparts_ready, 1)
            dve.wait_ge(sparts_ready, 2)
            dve.tensor_tensor(spt[2], pos, spt[1], ALU.subtract).then_inc(sparts_ready, 1)
            link(dve.tensor_scalar(cs[:, 5:6], v("cb2"), -1.0, None, ALU.mult))
            link(dve.tensor_tensor(cs[:, 5:6], cs[:, 5:6], v("cb2"), ALU.max))
            link(dve.tensor_scalar(cs[:, 6:7], v("cw3"), -1.0, None, ALU.mult))
            link(dve.tensor_tensor(cs[:, 6:7], cs[:, 6:7], v("cw3"), ALU.max))
            dve.wait_ge(bound_ready, 1)
            link(dve.tensor_tensor(cs[:, 7:8], bank(0)[:, 0:1], cs[:, 5:6], ALU.add))
            link(dve.tensor_tensor(cs[:, 7:8], cs[:, 7:8], cs[:, 6:7], ALU.mult))
            link(dve.tensor_scalar(cs[:, 7:8], cs[:, 7:8], 2.0 ** -40, None, ALU.max))
            link(dve.tensor_scalar(cs[:, 7:8].bitcast(i32), cs[:, 7:8].bitcast(i32), 0x7F800000, None, ALU.bitwise_and))
            link(dve.reciprocal(cs[:, 8:9], cs[:, 7:8]))
            link(dve.scalar_tensor_tensor(cs[:, 8:9], cs[:, 8:9], 2.0 ** 14, cs[:, 6:7], ALU.mult, ALU.mult))
            link(dve.tensor_tensor(cs[:, 9:10], v("cb2"), cs[:, 8:9], ALU.mult))
            link(dve.tensor_scalar(w2T[:, :], w2T[:, :], cs[:, 8:9], None, ALU.mult))
            dve.sem_inc(w2s_ready, 1)
            dve.wait_ge(cleared, 5)
            link(dve.memset(w3s[:, :], 0.0))
            link(dve.tensor_scalar(cs[:, 10:11], v("cw3"), 0.0, None, ALU.is_gt))
            link(dve.tensor_scalar(cs[:, 11:12], v("cw3"), 0.0, None, ALU.is_lt))
            link(dve.tensor_tensor(cs[:, 10:11], cs[:, 10:11], cs[:, 11:12], ALU.subtract))
            for h in range(2):
                a, b = CH * h, CH * (h + 1)
                link(dve.scalar_tensor_tensor(w3s[a:b, P - 1 + 8 * h:P + 8 * h], cs[a:b, 7:8], 2.0 ** -14, cs[a:b, 10:11], ALU.mult, ALU.mult))
            dve.wait_ge(w2sT_ready, 1)
            link(dve.tensor_copy(w2h[:, :], bank(0)[:, 0:P]))
            dve.tensor_tensor(w2l[:, :], bank(0)[:, 0:P], w2h[:, :].bitcast(fp32), ALU.subtract).then_inc(w2_ready, 1)
            dve.wait_ge(hat_ready, 1)
            for k in range(WS_POOL, NK):
                dve.wait_ge(hat_ready, k + 2)
                dve.tensor_tensor(wsm[:, k, :], wsm[:, k, :], hx[:, :], ALU.mult).then_inc(ws_ready, 1)

            def low1(m):
                dve.scalar_tensor_tensor(h1l[:, m % RING, :], z1[m % RING], 0.0, h1h[:, m % RING, :].bitcast(fp32),
                                         ALU.max, ALU.subtract).then_inc(h1l_ready, 1)

            def high2(m):
                dve.tensor_copy(h2h[m % RING], h2[m % RING]).then_inc(h2h_ready, 1)

            dve.sem_inc(bias_saved, 1)
            for m in range(RING):
                dve.wait_ge(h1h_ready, m + 1)
                low1(m)
            for m in range(AHEAD2):
                dve.wait_ge(h2_ready, m + 1)
                high2(m)
                dve.wait_ge(h1h_ready, m + RING + 1)
                low1(m + RING)
            with dve.Fori(0, G) as g:
                for m in range(AHEAD2, STEPS + AHEAD2):
                    dve.wait_ge(h2_ready, STEPS * g + m + 1)
                    high2(m)
                    dve.wait_ge(h1h_ready, STEPS * g + m + RING + 1)
                    low1(m + RING)
                    if m % RING == RING - 1:
                        dve.wait_ge(h2h_ready, STEPS * g + m + 1)
                        dve.tensor_tensor(h2l[m % RING], h2[m % RING], h2h[m % RING], ALU.subtract).then_inc(h2l_dve, 1)
                dve.wait_ge(bias_ready, g + 1)
                dve.tensor_copy(BT[:, g, :], bank(4)).then_inc(bias_saved, 1)
            dve.wait_ge(bias_saved, G + 1)

            shape = (P, NK, J)
            for u in range(G + 1):
                if u < G:
                    sim = bank(u % 2).rearrange("p (i j) -> p i j", j=J)
                    dve.wait_ge(qk_ready, u + 1)
                    dve.tensor_reduce(smax[u % 2][:, :], sim, AX.X, ALU.max).then_inc(max_found, 1)
                if u >= 1:
                    pr = prob[(u - 1) % 4].rearrange("p (i j) -> p i j", j=J)
                    dve.wait_ge(exped, u)
                    dve.tensor_reduce(ssum[(u - 1) % 2][:, :], pr, AX.X, ALU.add).then_inc(sum_found, 1)
                if u < G:
                    dve.wait_ge(max_found, u + 1)
                    dve.tensor_scalar(smax[u % 2][:, :], smax[u % 2][:, :], v("cb3"), None, ALU.add).then_inc(max_moved, 1)
                if u >= 1:
                    dve.wait_ge(sum_found, u)
                    if u >= 3:
                        dve.wait_ge(normed, u - 2)
                    dve.reciprocal(srec[(u - 1) % 2][:, :], ssum[(u - 1) % 2][:, :]).then_inc(sum_inverted, 1)
                if u < G:
                    if u >= 4:
                        dve.wait_ge(aT_ready, u - 3)
                    dve.wait_ge(max_moved, u + 1)
                    dve.scalar_tensor_tensor(prob[u % 4].rearrange("p (i j) -> p i j", j=J), sim, v("cb3"),
                                             smax[u % 2][:, :].unsqueeze(2).to_broadcast(shape), ALU.add, ALU.subtract).then_inc(shifted, 1)
            for n in range(T):
                b, hf = n // 2, n % 2
                for ct in range(CT):
                    r = CT * n + ct
                    xs = X[:, CT * b + ct, HALF * hf:HALF * (hf + 1)]
                    dve.wait_ge(y_ready, r + 1)
                    dve.scalar_tensor_tensor(xs, bank(r % 4), v("out_b", ct), xs, ALU.add, ALU.add).then_inc(x1_ready, 1)
            for n in range(T):
                b, hf = n // 2, n % 2
                for ct in range(CT):
                    r = CT * n + ct
                    xs = X[:, CT * b + ct, HALF * hf:HALF * (hf + 1)]
                    dve.wait_ge(m_ready, r + 1)
                    dve.wait_ge(xn2_ready, r + 1)
                    dve.scalar_tensor_tensor(xs, bank(4 + r % 4), v("mlp_b2", ct), xs, ALU.add, ALU.add).then_inc(x2_ready, 1)
            for n in range(2 * NK):
                b, jt = n // NK, n % NK
                dve.wait_ge(vv_ready, n + 1)
                dve.tensor_tensor(V[:, NH * b:NH * (b + 1), jt, :], bank(4 + n % 4)[:, 0:C].rearrange("p (n d) -> p n d", d=D),
                                  bv[:, :, :], ALU.add).then_inc(vv_saved, 1)
            def v_part(n, b):
                nn = slice(NH * b, NH * (b + 1))
                v0, vr = (x[:, nn, :, :].rearrange("p n j d -> p (n j) d") for x in (V, VR))
                v3 = [V3[:, nn, :, D * a:D * (a + 1)].rearrange("p n j d -> p (n j) d") for a in range(3)]
                if n > 0:
                    dve.wait_ge(v_done, 4 * b + n)
                if n == 0:
                    ins = dve.tensor_scalar(v3[0], v0, 1.0 / PSCALE, None, ALU.mult)
                elif n == 1:
                    ins = dve.scalar_tensor_tensor(vr, v0, 1.0 / PSCALE, v3[0], ALU.mult, ALU.subtract)
                elif n == 2:
                    ins = dve.tensor_copy(v3[1], vr)
                else:
                    ins = dve.tensor_tensor(v3[2], vr, v3[1], ALU.subtract)
                ins.then_inc(v_done, 1)

            dve.wait_ge(qw_scaled, 2)
            dve.wait_ge(vv_saved, 2 * NK)
            for n in range(2 * T):
                which, t = n % 2, n // 2
                i = n % 2
                dve.wait_ge(f_hi, n + 1)
                dve.scalar_tensor_tensor(part[i][1], bank(2 * i, 2), v(("bq", "bk")[which], t % CT), part[i][0].bitcast(fp32),
                                         ALU.add, ALU.subtract).then_inc(f_lo, 1)
                v_part(n % 4, n // 4)
            def maxes(u):
                dve.tensor_reduce(aneg[u % 2][:, :], bank(2 * (u % 2), 2), AX.X, ALU.max, negate=True).then_inc(mx_ready, 1)

            def high0T(u):
                dve.tensor_copy(PTH[u % 2][:, 0:HALF], PF[u % 2]).then_inc(pFh_ready, 1)

            def low1T(u):
                dve.scalar_tensor_tensor(PTL[u % 2][:, HALF:N], bank(5), PSCALE, PTH[u % 2][:, HALF:N],
                                         ALU.mult, ALU.subtract).then_inc(pTl_ready, 1)

            def inverse(u, k):
                dve.wait_ge(oo_ready, UNITS * k + u + 1)
                dve.wait_ge(oo_saved, UNITS * k + u + 1)
                dve.reciprocal(arec[u % 2][:, :], bank(6 + u % 2)[:, 3 * D:VW]).then_inc(rec_done, 1)

            for u in range(3):
                dve.wait_ge(sc_ready, u + 1)
                if u == 2:
                    dve.wait_ge(pr_ready, 1)
                maxes(u)
            dve.wait_ge(pF_ready, 1)
            high0T(0)
            dve.wait_ge(pTh_ready, 1)
            low1T(0)
            with dve.Fori(0, G // 2) as k:
                for i in range(UNITS):
                    if i >= 1:
                        inverse(i - 1, k)
                    dve.wait_ge(sc_ready, UNITS * k + i + 4)
                    dve.wait_ge(pr_ready, UNITS * k + i + 2)
                    maxes(i + 3)
                    dve.wait_ge(pF_ready, UNITS * k + i + 2)
                    high0T(i + 1)
                    dve.wait_ge(pTh_ready, UNITS * k + i + 2)
                    low1T(i + 1)
                inverse(UNITS - 1, k)
            for n in range(2 * T):
                b, ct, hf = n // 4, n // 2 % 2, n % 2
                xs = X[:, CT * b + ct, HALF * hf:HALF * (hf + 1)]
                dve.wait_ge(fin_ready, n + 1)
                dve.scalar_tensor_tensor(xs, bank(4 + n % 4), v("b_out", ct), xs, ALU.add, ALU.add).then_inc(fin_saved, 1)

        @block.tensor
        def _(pe):
            pe.wait_ge(ld_bd, 16 * (3 * HP + 4))
            for t in range(T):
                pe.wait_ge(xn_ready, t + 1)
                for hf in range(2):
                    pe.matmul(bank(2 * t + hf), qw[:, t % CT, :], XN[:, t, HALF * hf:HALF * (hf + 1)],
                              start=True, stop=True).then_inc(q_ready, 1)
            pe.wait_ge(ld_vec, 64)
            for r in range(2 * T):
                pe.wait_ge(q_saved, r + 1)
                for i in range(4):
                    k = 4 * (r % 2) + i
                    last = pe.transpose(bank(r)[:, P * i:P * (i + 1)], XN[:, r // 2, P * k:P * (k + 1)], ident[:, :])
                last.then_inc(xT_ready, 1)
            pe.wait_ge(gelu_ready, 1)
            pe.wait_ge(pwl_ready, 1)
            pe.wait_ge(xT_saved, 2 * T)
            for t in range(T):
                last = pe.matmul(ps[0:2 * G, 0:J], pwl[:, t, :, :].rearrange("p c g -> p (c g)"), gel[:, 9 * t:9 * t + KD, :],
                                 start=(t == 0), stop=(t == T - 1))
            last.then_inc(pw_ready, 1)
            pe.wait_ge(bound_in, 1)
            pe.matmul(bank(0)[:, 0:1], w2l[:, :].bitcast(fp32), cs[:, 4:5], start=True, stop=True).then_inc(bound_ready, 1)
            pe.wait_ge(w2s_ready, 1)
            pe.wait_ge(ld_vec, 64)
            pe.transpose(bank(0)[:, 0:P], w2T[:, :], ident[:, :]).then_inc(w2sT_ready, 1)
            for k in range(NK):
                if k < WS_POOL:
                    pe.wait_ge(ws_pool, k + 1)
                else:
                    pe.wait_ge(ws_ready, k + 1 - WS_POOL)
                for t in range(T):
                    for h in range(HP):
                        g = HP * t + h
                        last = pe.matmul(ps[D * h:D * (h + 1), 512 + J * t:512 + J * (t + 1)],
                                         xnT[:, t, P * k + D * h:P * k + D * (h + 1)], wsm[:, k, J * g:J * (g + 1)],
                                         start=(k == 0 and t == 0), stop=(k == NK - 1), skip_group_check=True)
            last.then_inc(kv_ready, 1)
            pe.wait_ge(kv_saved, 1)
            for t in range(T):
                last = pe.matmul(bank(2)[:, J * t:J * (t + 1)], kw[:, t % CT, :], kvs[:, t, :], start=True, stop=True)
            last.then_inc(k_ready, 1)
            for t in range(T):
                for i in range(2):
                    last = pe.matmul(bank(3)[J * i:J * (i + 1), P * t:P * (t + 1)], kvs[:, t, :], vw[:, t % CT, :],
                                     start=True, stop=True)
            last.then_inc(v_ready, 1)
            def layer1(m, g):
                c, q, hf = m // 8, m % 8 // 2, m % 2
                if m % 8 == 0:
                    pe.wait_ge(mv_ready, CHUNKS * g + c + 1)
                pe.matmul(z1[m % RING], wl1[32 * q:32 * q + ROWS, :], mv[c % 2][32 * q:32 * q + ROWS, HALF * hf:HALF * (hf + 1)],
                          start=True, stop=True).then_inc(z1_ready, 1)

            def layer2(m, g):
                pe.wait_ge(h1l_ready, STEPS * g + m + 1)
                pe.matmul(z2[m % 2], w2h[:, :], h1h[:, m % RING, :], start=True, stop=False)
                pe.matmul(z2[m % 2], w2h[:, :], h1l[:, m % RING, :], start=False, stop=False)
                pe.matmul(z2[m % 2], w2l[:, :], h1h[:, m % RING, :], start=False, stop=True).then_inc(z2_ready, 1)

            def layer3(m, g):
                c, q, hf = m // 8, m % 8 // 2, m % 2
                if m % RING == RING - 1:
                    pe.wait_ge(h2l_dve, STEPS // RING * g + (m + 1) // RING)
                else:
                    pe.wait_ge(h2l_pool, (STEPS - STEPS // RING) * g + m + 1 - (m + 1) // RING)
                a = P - 1 - (J * hf + 16 * q + c)
                pe.matmul(bank(4), w3s[:, a:a + P], h2h[m % RING], start=(m == 0), stop=False)
                return pe.matmul(bank(4), w3s[:, a:a + P], h2l[m % RING], start=False, stop=(m == STEPS - 1))

            pe.wait_ge(w1_in, 16 * (4 * NR + 6))
            pe.wait_ge(w2_ready, 1)
            pe.wait_ge(v_ready, 1)
            for m in range(RING):
                layer1(m, 0)
            for m in range(AHEAD2):
                if m >= 2:
                    pe.wait_ge(h2_ready, m - 1)
                layer2(m, 0)
                layer1(m + RING, 0)
            with pe.Fori(0, G) as g:
                for i in range(STEPS):
                    pe.wait_ge(h2_ready, STEPS * g + i + AHEAD2 - 1)
                    layer2(i + AHEAD2, g)
                    layer1(i + AHEAD1, g)
                    if i == 0:
                        pe.wait_ge(bias_saved, g + 1)
                    last = layer3(i, g)
                last.then_inc(bias_ready, 1)

            def sims(u):
                t, i = u // 4, u % 4
                if u >= 2:
                    pe.wait_ge(shifted, u - 1)
                sim = bank(u % 2).rearrange("p (f h j) -> p f h j", f=2, h=HP)
                for h in range(HP):
                    pe.matmul(sim[:, :, h, :], BT[:, HP * t + h, P * i:P * (i + 1)], ident[:, :],
                              start=(h == 0), stop=False, skip_group_check=True)
                for hf in range(2):
                    last = pe.matmul(bank(u % 2)[:, 256 * hf:256 * (hf + 1)], XN[:, t, P * (4 * hf + i):P * (4 * hf + i + 1)],
                                     ks[:, t, :, :].rearrange("p h j -> p (h j)"), start=False, stop=True, skip_group_check=True)
                last.then_inc(qk_ready, 1)

            def values(t):
                pe.wait_ge(aT_saved, 4 * (t + 1))
                if t >= 2:
                    pe.wait_ge(o_saved, t - 1)
                for hf in range(2):
                    for c in range(2):
                        a = 512 * (4 + 2 * (t % 2) + hf)
                        last = pe.matmul(ps[2 * D * c:2 * D * (c + 1), a:a + HALF], vs[:, t, c, :], att[t % 2][:, hf, c, :],
                                         start=True, stop=True)
                last.then_inc(o_ready, 1)

            pe.wait_ge(h1l_ready, STEPS * G + AHEAD1)
            pe.wait_ge(h2_ready, STEPS * G + AHEAD2)
            pe.wait_ge(h2l_pool, (STEPS - STEPS // RING) * G + AHEAD2)
            pe.wait_ge(bias_saved, G + 1)
            pe.wait_ge(q_copied, T)
            pe.wait_ge(k_saved, HP)
            pe.wait_ge(v_saved, 2)
            sims(0)
            sims(1)
            for u in range(G):
                if u + 2 < G:
                    sims(u + 2)
                if u % 4 == 0 and u > 0:
                    values(u // 4 - 1)
                pe.wait_ge(normed, u + 1)
                if u >= 2:
                    pe.wait_ge(aT_saved, u - 1)
                for i in range(4):
                    last = pe.transpose(bank(2 + u % 2)[:, P * i:P * (i + 1)], prob[u % 4][:, P * i:P * (i + 1)], ident[:, :])
                last.then_inc(aT_ready, 1)
            values(T - 1)
            pe.wait_ge(ld_late, 16 * 6)
            pe.wait_ge(o_saved, T)
            for n in range(T):
                b, hf = n // 2, n % 2
                for ct in range(CT):
                    r = CT * n + ct
                    if r >= 4:
                        pe.wait_ge(x1_ready, r - 3)
                    for kt in range(CT):
                        last = pe.matmul(bank(r % 4), outw[:, kt, P * ct:P * (ct + 1)], ao[:, CT * b + kt, HALF * hf:HALF * (hf + 1)],
                                         start=(kt == 0), stop=(kt == CT - 1))
                    last.then_inc(y_ready, 1)
            pe.wait_ge(x1_ready, 2 * T)
            for n in range(T):
                b, hf = n // 2, n % 2
                pe.wait_ge(xn2_ready, CT * (n + 1))
                for f in range(FT):
                    r = FT * n + f
                    if r >= 4:
                        pe.wait_ge(hid_saved, r - 3)
                    for kt in range(CT):
                        last = pe.matmul(bank(f % 4), m1[:, kt, P * f:P * (f + 1)], XN[:, CT * b + kt, HALF * hf:HALF * (hf + 1)],
                                         start=(kt == 0), stop=(kt == CT - 1))
                    last.then_inc(hid_ready, 1)
                for ct in range(CT):
                    r = CT * n + ct
                    if r >= 4:
                        pe.wait_ge(x2_ready, r - 3)
                    for f in range(FT):
                        if ct == 0:
                            pe.wait_ge(hid_saved, FT * n + f + 1)
                        last = pe.matmul(bank(4 + r % 4), m2[:, f, P * ct:P * (ct + 1)], hm[:, f, :],
                                         start=(f == 0), stop=(f == FT - 1))
                    last.then_inc(m_ready, 1)

            pe.wait_ge(x2_ready, 2 * T)
            wv = wqkv[:, :, :].rearrange("p t (k n) -> p t k n", k=3)
            for n in range(2 * NK):
                b, jt = n // NK, n % NK
                if n >= 4:
                    pe.wait_ge(vv_saved, n - 3)
                for kt in range(CT):
                    last = pe.matmul(bank(4 + n % 4)[:, 0:C], X[:, CT * b + kt, P * jt:P * (jt + 1)], wv[:, kt, 2, :],
                                     start=(kt == 0), stop=(kt == CT - 1))
                last.then_inc(vv_ready, 1)
            pe.wait_ge(qw_scaled, 2)
            for n in range(2 * T):
                which, t = n % 2, n // 2
                b, mt = t // CT, t % CT
                if n >= 2:
                    pe.wait_ge(f_lo, n - 1)
                for hf in range(2):
                    for kt in range(CT):
                        last = pe.matmul(bank(2 * (n % 2) + hf), wv[:, kt, which, P * mt:P * (mt + 1)],
                                         X[:, CT * b + kt, HALF * hf:HALF * (hf + 1)], start=(kt == 0), stop=(kt == CT - 1))
                last.then_inc(p_ready, 1)

            def scores(u):
                i, it = u // NK % 2, u % NK
                for jh in range(2):
                    last = pe.matmul(bank(2 * (u % 2) + jh), QS[i][:, P * it:P * (it + 1)], KS[i][:, HALF * jh:HALF * (jh + 1)],
                                     start=True, stop=True)
                last.then_inc(sc_ready, 1)

            def turn(u, hf):
                for i in range(4):
                    jt = 4 * hf + i
                    last = pe.transpose(bank(4 + hf)[:, P * i:P * (i + 1)], PR[u % 2][:, P * jt:P * (jt + 1)], ident[:, :])
                last.then_inc(pT_ready, 1)

            def weigh(u, k):
                order = list(range(4, NK)) + list(range(4))
                for jt in order:
                    for pT in (PTH, PTL):
                        last = pe.matmul(bank(6 + u % 2)[:, 0:VW], pT[u % 2][:, P * jt:P * (jt + 1)],
                                         V3[:, 2 * k + u // NK, jt, :],
                                         start=(jt == order[0] and pT is PTH), stop=(jt == order[-1] and pT is PTL))
                last.then_inc(oo_ready, 1)

            pe.wait_ge(f_lo, 2 * T)
            pe.wait_ge(st_in[0], 16 * 2 * HP)
            scores(0)
            scores(1)
            pe.wait_ge(pr_ready, 1)
            scores(2)
            turn(0, 0)
            turn(0, 1)
            pe.wait_ge(sums_column, 1)
            pe.wait_ge(v_done, 4 * B)
            with pe.Fori(0, G // 2) as k:
                for i in range(UNITS):
                    if i + 3 == NK:
                        pe.wait_ge(st_in[1], 16 * 2 * HP * (k + 1))
                    if i + 3 == UNITS:
                        pe.wait_ge(st_in[0], 16 * 2 * HP * (k + 2))
                    pe.wait_ge(pr_ready, UNITS * k + i + 2)
                    scores(i + 3)
                    pe.wait_ge(pF_ready, UNITS * k + i + 1)
                    turn(i + 1, 0)
                    pe.wait_ge(pTl_ready, UNITS * k + i + 1)
                    turn(i + 1, 1)
                    pe.wait_ge(oo_saved, UNITS * k + i + 1)
                    pe.wait_ge(pFl_ready, UNITS * k + i + 2)
                    weigh(i, k)
            pe.wait_ge(o_done, UNITS * (G // 2) + 2)
            pe.wait_ge(pTl_ready, UNITS * (G // 2) + 1)
            for n in range(2 * T):
                t, hf = n // 2, n % 2
                b, ct = t // CT, t % CT
                if n >= 4:
                    pe.wait_ge(rT_saved, n - 3)
                for i in range(4):
                    last = pe.transpose(bank(n % 4)[:, P * i:P * (i + 1)],
                                        RES[:, 4 * hf + i, NH * b + HP * ct:NH * b + HP * (ct + 1), :].rearrange("p n d -> p (n d)"),
                                        ident[:, :])
                last.then_inc(rT_ready, 1)
            for n in range(2 * T):
                b, ct, hf = n // 4, n // 2 % 2, n % 2
                pe.wait_ge(rT_saved, 4 * b + 4)
                if n >= 4:
                    pe.wait_ge(fin_saved, n - 3)
                for kt in range(CT):
                    last = pe.matmul(bank(4 + n % 4), wout[:, kt, P * ct:P * (ct + 1)], rT[:, CT * b + kt, HALF * hf:HALF * (hf + 1)],
                                     start=(kt == 0), stop=(kt == CT - 1))
                last.then_inc(fin_ready, 1)


def kernel(**inputs):
    import numpy as _np
    import concourse.bacc as _bacc
    from concourse import mybir as _mybir
    from concourse.bass_utils import run_bass_kernel_spmd as _run

    a = {k: _np.asarray(v) for k, v in inputs.items()}
    L0, L1 = "L0_conv_", "L1_conv_"

    def col(x):
        return x.reshape(-1, P).T

    def rep(x, n):
        return _np.tile(x, (n, 1))

    bqkv = a[L1 + "b_qkv"].reshape(NH, 3, D)
    part = _np.arange(P)
    vecs = _np.concatenate([
        col(a[L0 + "bn1_g"]), col(a[L0 + "bn1_b"]), col(a[L0 + "bn2_g"]), col(a[L0 + "bn2_b"]), col(a[L0 + "out_b"]),
        col(a[L0 + "mlp_b2"]), col(a[L1 + "b_out"]), col(a[L0 + "mlp_b1"]),
        rep(a[L0 + "off_dw_w"].reshape(D, TAPS * TAPS), HP), rep(a[L0 + "off_dw_b"].reshape(D, 1), HP),
        rep(a[L0 + "cpb_b1"].reshape(CH, 1), 2), rep(a[L0 + "cpb_b2"].reshape(CH, 1), 2),
        rep(a[L0 + "cpb_w1"].T, 2), rep(a[L0 + "cpb_w3"], 2), (part % 32 // 3 == 4).astype(_np.float32).reshape(P, 1),
        rep(a[L0 + "cpb_b3"].reshape(1, 1), P),
        rep(a[L0 + "off_pw_w"].T, HP), col(bqkv[:, 0].reshape(-1)), col(bqkv[:, 1].reshape(-1)),
        (part % W).reshape(P, 1).astype(_np.float32),
        (4 * _np.arange(NK)[None, :] + (part // W)[:, None]).astype(_np.float32)], axis=1)
    j = _np.arange(J)
    gq = (2.0 * _np.arange(W, dtype=_np.float32) / _np.float32(W - 1) - 1.0).astype(_np.float32)
    arrays = {
        "x": a["x"].reshape(B, C, N), "vecs": vecs, "ident": _np.eye(P, dtype=_np.float32),
        "gridj": _np.concatenate([_np.tile(j % KD, (G, 1)), _np.tile(j // KD, (G, 1))]).astype(_np.float32),
        "gridq": _np.tile(gq, (2 * G, 1)),
        "qwT": a[L0 + "qw"].transpose(0, 2, 1), "kwT": a[L0 + "kw"].transpose(0, 2, 1), "vwT": a[L0 + "vw"].transpose(0, 2, 1),
        "cw1": _np.concatenate([a[L0 + "cpb_w1"], a[L0 + "cpb_b1"].reshape(1, CH)]), "cw2": a[L0 + "cpb_w2"], "cw2T": a[L0 + "cpb_w2"].T,
        "out_wT": a[L0 + "out_w"].T, "m1T": a[L0 + "mlp_w1"].T, "m2T": a[L0 + "mlp_w2"].T,
        "wqkv": a[L1 + "W_qkv"].reshape(C, NH, 3, D).transpose(0, 2, 1, 3).reshape(C, 3 * C), "wout": a[L1 + "W_out"], "bv": bqkv[:, 2],
    }
    arrays = {k: _np.ascontiguousarray(v) for k, v in arrays.items()}
    nc = _bacc.Bacc("TRN2", target_bir_lowering=False, num_devices=1)
    d = {k: nc.dram_tensor("in_" + k, v.shape, _mybir.dt.from_np(v.dtype), kind="ExternalInput").ap() for k, v in arrays.items()}
    out = nc.dram_tensor("out", (B, C, N), _mybir.dt.float32, kind="ExternalOutput").ap()
    build(nc, d, out)
    r = _run(nc, [{"in_" + k: v for k, v in arrays.items()}], core_ids=[0])
    return _np.asarray(r.results[0]["out"]).reshape(B, C, H, W)
```
